# Optimizing a Trainium2 kernel written in Bass

```python
import numpy as np
import jax
import jax.numpy as jnp

def _softmax(x, axis=-1):
    return jax.nn.softmax(x, axis=axis)

def _gelu(x):
    return jax.nn.gelu(x, approximate=True)

def _silu(x):
    return jax.nn.silu(x)

def _sigmoid(x):
    return jax.nn.sigmoid(x)

def _layernorm(x, axis=-1, eps=1e-05):
    m = jnp.mean(x, axis=axis, keepdims=True)
    v = jnp.var(x, axis=axis, keepdims=True)
    return (x - m) / jnp.sqrt(v + eps)

def _scatter_add(tgt, idx, src, axis=0):
    return tgt.at[idx].add(src)

def _segment_sum(src, seg, n):
    return jax.ops.segment_sum(src, seg, n)
kernel_name = 'mk_decoder_preln_d1_seqx_r8_5b6403'

def setup_inputs(seed: int=0):
    np.random.seed(seed)
    _w = jnp.asarray

    def _rec_inputs():
        import jax
        import jax.numpy as jnp
        _rk = jax.random.key(seed)
        x = -0.0002928 + 1 * jax.random.normal(jax.random.fold_in(_rk, 1), (32, 128, 128), jnp.float32)
        _lenS = 128 - jax.random.randint(jax.random.fold_in(_rk, 7), (32,), 0, max(1, 128 // 4) + 1, jnp.int32)
        _lenS2 = 77 - jax.random.randint(jax.random.fold_in(_rk, 8), (32,), 0, max(1, 77 // 4) + 1, jnp.int32)
        _ctx_1024P = jax.random.normal(jax.random.fold_in(_rk, 11), (32, 16, 128), jnp.float32)
        _ctx_1024c = jax.random.dirichlet(jax.random.fold_in(_rk, 511), 0.3 * jnp.ones((16,), jnp.float32), (32, 77))
        _ctx_1024t = jnp.einsum('bsk,bkd->bsd', _ctx_1024c, _ctx_1024P)
        _ctx_1024t = _ctx_1024t * jax.lax.rsqrt(jnp.mean(jnp.square(_ctx_1024t)) + 1e-12) * 0.953939
        ctx_1024 = -1.39393e-06 + 0.999914 * (_ctx_1024t + 0.3 * jax.random.normal(jax.random.fold_in(_rk, 611), (32, 77, 128), jnp.float32))
        return (x, ctx_1024)
    x, ctx_1024 = _rec_inputs()

    def _L0_attn_setup():
        import jax, jax.numpy as jnp
        import numpy as np
        B, L, D, H = (2, 256, 128, 16)
        HD = D // H
        ROPE_BASE = 10000.0

        def _rope(x):
            seq, hd = (x.shape[2], x.shape[3])
            inv_freq = 1.0 / ROPE_BASE ** (jnp.arange(0, hd, 2, dtype=jnp.float32) / hd)
            freqs = jnp.arange(seq, dtype=jnp.float32)[:, None] * inv_freq
            cos = jnp.repeat(jnp.cos(freqs), 2, axis=-1)
            sin = jnp.repeat(jnp.sin(freqs), 2, axis=-1)
            xp = x.reshape(*x.shape[:-1], hd // 2, 2)
            x_rot = jnp.stack([-xp[..., 1], xp[..., 0]], axis=-1).reshape(x.shape)
            return x * cos + x_rot * sin
        key = jax.random.key(seed)
        ks = jax.random.split(key, 9)
        s = 1.0 / np.sqrt(D)
        mk = lambda k: jax.random.normal(k, (D, D), dtype=jnp.float32) * s
        return {'x': jax.random.normal(ks[0], (B, L, D), dtype=jnp.float32), 'Wq': mk(ks[1]), 'bq': jnp.zeros((D,), jnp.float32), 'Wk': mk(ks[2]), 'bk': jnp.zeros((D,), jnp.float32), 'Wv': mk(ks[3]), 'bv': jnp.zeros((D,), jnp.float32), 'Wp': mk(ks[4]), 'bp': jnp.zeros((D,), jnp.float32)}
    _L0_attn_all = _L0_attn_setup()
    _L0_attn_in = {k: v for k, v in _L0_attn_all.items() if k in ('Wq', 'bq', 'Wk', 'bk', 'Wv', 'bv', 'Wp', 'bp')}
    del _L0_attn_all

    def _L0_xattn_setup():
        import jax, jax.numpy as jnp
        import numpy as np
        D_MODEL = 128
        N_HEAD = 16
        D_K = D_MODEL // N_HEAD

        def _split_heads(x):
            B, S, _ = x.shape
            return x.reshape(B, S, N_HEAD, D_K).transpose(0, 2, 1, 3)
        key = jax.random.key(seed)
        ks = jax.random.split(key, 11)
        B, S = (2, 256)
        scale = 1.0 / np.sqrt(D_MODEL)
        inp = {'q': jax.random.normal(ks[0], (B, S, D_MODEL), jnp.float32), 'k': jax.random.normal(ks[1], (B, S, D_MODEL), jnp.float32), 'v': jax.random.normal(ks[2], (B, S, D_MODEL), jnp.float32), 'Wq': jax.random.normal(ks[3], (D_MODEL, D_MODEL), jnp.float32) * scale, 'bq': jnp.zeros((D_MODEL,), jnp.float32), 'Wk': jax.random.normal(ks[4], (D_MODEL, D_MODEL), jnp.float32) * scale, 'bk': jnp.zeros((D_MODEL,), jnp.float32), 'Wv': jax.random.normal(ks[5], (D_MODEL, D_MODEL), jnp.float32) * scale, 'bv': jnp.zeros((D_MODEL,), jnp.float32), 'Wo': jax.random.normal(ks[6], (D_MODEL, D_MODEL), jnp.float32) * scale, 'bo': jnp.zeros((D_MODEL,), jnp.float32)}
        return inp
    _L0_xattn_all = _L0_xattn_setup()
    _L0_xattn_in = {k: v for k, v in _L0_xattn_all.items() if k in ('Wq', 'bq', 'Wk', 'bk', 'Wv', 'bv', 'Wo', 'bo')}
    del _L0_xattn_all

    def _L0_ffn_setup():
        import jax, jax.numpy as jnp
        import numpy as np
        D = 128
        H = 512
        E = 8
        B = 2
        T = 256
        LN_EPS = 1e-05

        def _layer_norm(r, gamma, beta):
            mu = jnp.mean(r, axis=-1, keepdims=True)
            var = jnp.mean(jnp.square(r - mu), axis=-1, keepdims=True)
            return (r - mu) * jax.lax.rsqrt(var + LN_EPS) * gamma + beta
        key = jax.random.key(seed)
        ks = jax.random.split(key, 9)
        s_in = 1.0 / np.sqrt(D)
        s_hid = 1.0 / np.sqrt(H)
        x = jax.random.normal(ks[0], (B, T, D), dtype=jnp.float32)
        Wg = jax.random.uniform(ks[1], (D, E), jnp.float32, -s_in, s_in)
        bg = jax.random.uniform(ks[2], (E,), jnp.float32, -s_in, s_in)
        W1 = jax.random.uniform(ks[3], (E, D, H), jnp.float32, -s_in, s_in)
        b1 = jax.random.uniform(ks[4], (E, H), jnp.float32, -s_in, s_in)
        W2 = jax.random.uniform(ks[5], (E, H, D), jnp.float32, -s_hid, s_hid)
        b2 = jax.random.uniform(ks[6], (E, D), jnp.float32, -s_hid, s_hid)
        gamma = jnp.ones((D,), jnp.float32)
        beta = jnp.zeros((D,), jnp.float32)
        return {'x': x, 'Wg': Wg, 'bg': bg, 'W1': W1, 'b1': b1, 'W2': W2, 'b2': b2, 'gamma': gamma, 'beta': beta}
    _L0_ffn_all = _L0_ffn_setup()
    _L0_ffn_in = {k: v for k, v in _L0_ffn_all.items() if k in ('Wg', 'bg', 'W1', 'b1', 'W2', 'b2', 'gamma', 'beta')}
    del _L0_ffn_all
    return {'x': x, 'ctx_1024': ctx_1024, 'L0_attn_Wq': _L0_attn_in['Wq'], 'L0_attn_bq': _L0_attn_in['bq'], 'L0_attn_Wk': _L0_attn_in['Wk'], 'L0_attn_bk': _L0_attn_in['bk'], 'L0_attn_Wv': _L0_attn_in['Wv'], 'L0_attn_bv': _L0_attn_in['bv'], 'L0_attn_Wp': _L0_attn_in['Wp'], 'L0_attn_bp': _L0_attn_in['bp'], 'L0_xattn_Wq': _L0_xattn_in['Wq'], 'L0_xattn_bq': _L0_xattn_in['bq'], 'L0_xattn_Wk': _L0_xattn_in['Wk'], 'L0_xattn_bk': _L0_xattn_in['bk'], 'L0_xattn_Wv': _L0_xattn_in['Wv'], 'L0_xattn_bv': _L0_xattn_in['bv'], 'L0_xattn_Wo': _L0_xattn_in['Wo'], 'L0_xattn_bo': _L0_xattn_in['bo'], 'L0_ffn_Wg': _L0_ffn_in['Wg'], 'L0_ffn_bg': _L0_ffn_in['bg'], 'L0_ffn_W1': _L0_ffn_in['W1'], 'L0_ffn_b1': _L0_ffn_in['b1'], 'L0_ffn_W2': _L0_ffn_in['W2'], 'L0_ffn_b2': _L0_ffn_in['b2'], 'L0_ffn_gamma': _L0_ffn_in['gamma'], 'L0_ffn_beta': _L0_ffn_in['beta']}

def reference(x, ctx_1024, L0_attn_Wq, L0_attn_bq, L0_attn_Wk, L0_attn_bk, L0_attn_Wv, L0_attn_bv, L0_attn_Wp, L0_attn_bp, L0_xattn_Wq, L0_xattn_bq, L0_xattn_Wk, L0_xattn_bk, L0_xattn_Wv, L0_xattn_bv, L0_xattn_Wo, L0_xattn_bo, L0_ffn_Wg, L0_ffn_bg, L0_ffn_W1, L0_ffn_b1, L0_ffn_W2, L0_ffn_b2, L0_ffn_gamma, L0_ffn_beta):
    import jax
    import jax.numpy as jnp

    def _L0_attn_ref(x, Wq, bq, Wk, bk, Wv, bv, Wp, bp):
        import jax, jax.numpy as jnp
        import numpy as np
        B, L, D, H = (2, 256, 128, 16)
        HD = D // H
        ROPE_BASE = 10000.0

        def _rope(x):
            seq, hd = (x.shape[2], x.shape[3])
            inv_freq = 1.0 / ROPE_BASE ** (jnp.arange(0, hd, 2, dtype=jnp.float32) / hd)
            freqs = jnp.arange(seq, dtype=jnp.float32)[:, None] * inv_freq
            cos = jnp.repeat(jnp.cos(freqs), 2, axis=-1)
            sin = jnp.repeat(jnp.sin(freqs), 2, axis=-1)
            xp = x.reshape(*x.shape[:-1], hd // 2, 2)
            x_rot = jnp.stack([-xp[..., 1], xp[..., 0]], axis=-1).reshape(x.shape)
            return x * cos + x_rot * sin
        b, l, d = x.shape
        to_heads = lambda t: t.reshape(b, l, H, HD).transpose(0, 2, 1, 3)
        q = to_heads(x @ Wq + bq)
        k = to_heads(x @ Wk + bk)
        v = to_heads(x @ Wv + bv)
        q = _rope(q)
        k = _rope(k)
        scores = jnp.einsum('bhic,bhjc->bhij', q, k) / np.sqrt(HD)
        attn = jax.nn.softmax(scores, axis=-1)
        out = jnp.einsum('bhij,bhjc->bhic', attn, v)
        out = out.transpose(0, 2, 1, 3).reshape(b, l, d)
        return out @ Wp + bp

    def _L0_xattn_ref(q, k, v, Wq, bq, Wk, bk, Wv, bv, Wo, bo):
        import jax, jax.numpy as jnp
        import numpy as np
        D_MODEL = 128
        N_HEAD = 16
        D_K = D_MODEL // N_HEAD

        def _split_heads(x):
            B, S, _ = x.shape
            return x.reshape(B, S, N_HEAD, D_K).transpose(0, 2, 1, 3)
        qh = _split_heads(q @ Wq.T + bq)
        kh = _split_heads(k @ Wk.T + bk)
        vh = _split_heads(v @ Wv.T + bv)
        score = jnp.einsum('bhqd,bhkd->bhqk', qh, kh) / jnp.sqrt(jnp.float32(D_K))
        attn = jax.nn.softmax(score, axis=-1)
        out = jnp.einsum('bhqk,bhkd->bhqd', attn, vh)
        B, H, S, Dk = out.shape
        out = out.transpose(0, 2, 1, 3).reshape(B, S, H * Dk)
        return out @ Wo.T + bo

    def _L0_ffn_ref(x, Wg, bg, W1, b1, W2, b2, gamma, beta):
        import jax, jax.numpy as jnp
        import numpy as np
        D = 128
        H = 512
        E = 8
        B = 2
        T = 256
        LN_EPS = 1e-05

        def _layer_norm(r, gamma, beta):
            mu = jnp.mean(r, axis=-1, keepdims=True)
            var = jnp.mean(jnp.square(r - mu), axis=-1, keepdims=True)
            return (r - mu) * jax.lax.rsqrt(var + LN_EPS) * gamma + beta
        logits = jnp.einsum('btd,de->bte', x, Wg) + bg
        top2_vals, top2_idx = jax.lax.top_k(logits, 2)
        scores = jax.nn.softmax(top2_vals, axis=-1)
        onehot = jax.nn.one_hot(top2_idx, E, dtype=x.dtype)
        combine = jnp.einsum('btk,btke->bte', scores, onehot)
        h = jnp.einsum('btd,edh->bteh', x, W1) + b1[None, None]
        h = jax.nn.gelu(h, approximate=False)
        y = jnp.einsum('bteh,ehd->bted', h, W2) + b2[None, None]
        out = jnp.einsum('bted,bte->btd', y, combine)
        return _layer_norm(x + out, gamma, beta)
    x = x + _L0_attn_ref(_layernorm(x, axis=-1), L0_attn_Wq, L0_attn_bq, L0_attn_Wk, L0_attn_bk, L0_attn_Wv, L0_attn_bv, L0_attn_Wp, L0_attn_bp)
    x = x + _L0_xattn_ref(_layernorm(x, axis=-1), ctx_1024, ctx_1024, L0_xattn_Wq, L0_xattn_bq, L0_xattn_Wk, L0_xattn_bk, L0_xattn_Wv, L0_xattn_bv, L0_xattn_Wo, L0_xattn_bo)
    x = x + _L0_ffn_ref(_layernorm(x, axis=-1), L0_ffn_Wg, L0_ffn_bg, L0_ffn_W1, L0_ffn_b1, L0_ffn_W2, L0_ffn_b2, L0_ffn_gamma, L0_ffn_beta)
    return x

_drawn_inputs = setup_inputs


def setup_inputs(seed=0):
    import zlib

    import numpy as np

    out = dict(_drawn_inputs(seed))
    spreads = {'L0_attn_bq': (0.0, 0.561),
     'L0_attn_bk': (0.0, 0.639),
     'L0_attn_bv': (0.0, 0.1),
     'L0_attn_bp': (0.0, 0.1),
     'L0_xattn_bq': (0.0, 0.342),
     'L0_xattn_bk': (0.0, 0.8),
     'L0_xattn_bv': (0.0, 0.1),
     'L0_xattn_bo': (0.0, 0.1),
     'L0_ffn_gamma': (1.0, 0.2),
     'L0_ffn_beta': (0.0, 0.1)}
    factors = {'L0_ffn_bg': 3.588, 'L0_ffn_b1': 8.0, 'L0_ffn_b2': 6.479}
    for name, (base, spread) in spreads.items():
        noise = np.random.default_rng([zlib.crc32(name.encode()), seed]).standard_normal(out[name].shape)
        drawn = base * np.exp(spread * noise) if base else spread * noise
        out[name] = jnp.asarray(drawn.astype(out[name].dtype))
    for name, factor in factors.items():
        out[name] = (out[name] * factor).astype(out[name].dtype)
    return out
```

```python
import concourse.bass as bass
from concourse import mybir
from contextlib import ExitStack

F32 = mybir.dt.float32
F16 = mybir.dt.float16
BF16 = mybir.dt.bfloat16
I32 = mybir.dt.int32
U32 = mybir.dt.uint32
ALU = mybir.AluOpType
ACT = mybir.ActivationFunctionType
AX = mybir.AxisListType

P = 128
SEQS, L, D, LC = 32, 128, 128, 77
H, HD = 16, 8
GS = 4
NG = SEQS // GS
TOK = GS * L
CTOK = GS * LC
NJ, NB = 4, 4
VW = 32
INST = 2 * GS
SCALE = 1.0 / 8.0 ** 0.5
EPS = 1e-5
E, HID = 8, 512
NTOK = SEQS * L
TOPK = 2
HC = HID // P
REGION = NTOK + P
ROUND = 8
NT = -(-((NTOK * TOPK) // P + E - 1) // ROUND) * ROUND
PAYW = D + 2
SPARE = E * REGION
YROWS = TOPK * NTOK

BACKGROUND = {
    (2, 0): [("v2", 0, "own")], (2, 1): [("x2t0", 1, "q2")], (2, 2): [("q20", 0, "q2")], (2, 3): [("gq20", 1, "q2")],
    (3, 0): [("xnt", 0, "next")], (3, 1): [("x2t1", 1, "q2"), ("q", 0, "next")],
    (3, 2): [("q21", 0, "q2"), ("rq", 1, "next")], (3, 3): [("gq21", 1, "q2"), ("k", 0, "next")],
    (4, 0): [("rk", 1, "next")], (4, 1): [("x2t2", 1, "q2")], (4, 2): [("q22", 0, "q2")],
    (4, 3): [("v", 0, "next"), ("gq22", 1, "q2")],
    (5, 0): [("gq0", 0, "next")], (5, 1): [("gq1", 0, "next"), ("x2t3", 1, "q2")],
    (5, 2): [("gq2", 1, "next"), ("q23", 0, "q2")], (5, 3): [("gq3", 0, "next"), ("gq23", 1, "q2")],
    (6, 0): [("gk0", 0, "next")], (6, 1): [("gk1", 1, "next")], (6, 2): [("gk2", 0, "next"), ("x3t0", 1, "x3")],
    (6, 3): [("gk3", 0, "next")],
    (7, 2): [("x3t1", 1, "x3")],
    (0, 0): [("k2", 0, "own")], (0, 2): [("gk20", 0, "own"), ("x3t2", 1, "tail")], 
    (1, 0): [("x3t3", 1, "tail"), ("gk21", 0, "own")], (1, 1): [("log", 0, "tail"), ("gk22", 1, "own")],
    (1, 2): [("gk23", 0, "own")], (1, 3): [("pos", 1, "tail")],
}


def items_at(t, j, kinds):
    return [(n, b) for n, b, kind in BACKGROUND.get((t, j), []) if kind in kinds]


def order_of(steps, kinds_of):
    return [it for t in steps for j in range(NJ) for it in items_at(t, j, kinds_of(t))]


NEXT_ITEMS = [it for t in range(2, 8) for j in range(NJ) for it in items_at(t, j, ("next",))]
TAIL_ITEMS = order_of((0, 1), lambda t: ("tail",))
PRO_ORDER = NEXT_ITEMS + order_of((0, 1), lambda t: ("own",))
BODY_ORDER = order_of((2, 3, 4, 5, 6, 7), lambda t: ("q2", "next", "x3", "own")) + order_of((0, 1), lambda t: ("own", "tail"))
LAST_ORDER = order_of((2, 3, 4, 5, 6, 7), lambda t: ("q2", "x3", "own")) + order_of((0, 1), lambda t: ("tail",))


class Phase:

    def __init__(self, kind, g):
        self.kind, self.g = kind, g
        self.order = {"before": PRO_ORDER, "body": BODY_ORDER, "after": LAST_ORDER}[kind]

    def item(self, name):
        bank = dict(self.order)[name]
        on_bank = [n for n, b in self.order if b == bank]
        before = sum(b == bank for _, b in PRO_ORDER)
        body = sum(b == bank for _, b in BODY_ORDER)
        base = 0 if self.kind == "before" else self.g * body + before
        return bank, base + on_bank.index(name) + 1

    def kinds(self, t):
        if self.kind == "before":
            return ("own",)
        if t < 2:
            return ("own", "tail")
        return ("q2", "next", "x3", "own") if self.kind == "body" else ("q2", "x3", "own")

    def at(self, t, j):
        return [(n, kind) for n, _, kind in BACKGROUND.get((t, j), []) if kind in self.kinds(t)]


def decoder_layer(nc, x, ctx_t, w_self, b_self, bp, w_cross, b_cross, bo, wg, bg, w1, b1, w2, b2,
                  gamma, beta, cos_t, sin_t, sel_q, sel_k, ones_rows, ident, ident_bf, upper, ebase,
                  row_id, tile_edge, fill, out):
    stack = ExitStack()
    with stack:
        def sb(name, shape, dt=F32):
            return stack.enter_context(nc.sbuf_tensor(name, shape, dt))

        def pb(name, shape, dt=F32):
            return stack.enter_context(nc.psum_tensor(name, shape, dt))

        def sem(name):
            return stack.enter_context(nc.semaphore(name))

        x_rows = x.rearrange("(g i) l d -> l g i d", i=GS)
        out_rows = out.rearrange("s l d -> l s d")

        routed = nc.dram_tensor("routed", (SPARE + P, PAYW), F32, kind="Internal").ap()
        expert_out = nc.dram_tensor("expert_out", (YROWS + P, D), F32, kind="Internal").ap()

        wself = sb("wself", [P, 6, D])
        wcross = sb("wcross", [P, 4, D])
        bself = sb("bself", [P, 5])
        bcross = sb("bcross", [P, 3])
        cosb = sb("cosb", [P, L])
        sinb = sb("sinb", [P, L])
        selq = sb("selq", [P, 2, NB, P], F16)
        selk = sb("selk", [P, 2, NB, P], F16)
        onesr = sb("onesr", [P, NJ, NB, P], BF16)
        idf = sb("idf", [P, P])
        idb = sb("idb", [P, P], BF16)
        upperb = sb("upperb", [P, P], BF16)
        onesb = sb("onesb", [P, P], BF16)
        bprow = sb("bprow", [P, D])
        borow = sb("borow", [P, D])
        cself = sb("cself", [P, D])
        ccross = sb("ccross", [P, D])
        bvb = sb("bvb", [P, 2, P])
        wgs = sb("wgs", [P, E])
        bgrow = sb("bgrow", [P, E])
        etab = sb("etab", [P, 2, E])
        ebaser, iota8 = etab[:, 0, :], etab[:, 1, :]
        rowid = sb("rowid", [P, SEQS, TOPK], I32)
        half = sb("half", [P, GS])

        xin = sb("xin", [P, GS, D])
        ctxb = sb("ctxb", [P, CTOK])
        st1 = sb("st1", [P, GS, 6])
        mv1 = sb("mv1", [P, GS, 2])
        rs1 = sb("rs1", [P, GS])
        ve1 = sb("ve1", [P, GS])
        xn1 = sb("xn1", [P, GS, D])
        xc = sb("xc", [P, GS, D])
        xnt = sb("xnt", [P, TOK])
        ra = sb("ra", [P, 2, TOK])
        rb = sb("rb", [P, 2, TOK])
        rsum = sb("rsum", [P, 2, TOK])
        rhi = sb("rhi", [P, 2, TOK], F16)
        rlo = sb("rlo", [P, 2, TOK], F16)
        qs = sb("qs", [P, NB, TOK], F16)
        ks = sb("ks", [P, NB, TOK], F16)
        va = sb("va", [P, GS, H, VW])
        k2hi = sb("k2hi", [P, CTOK], F16)
        k2lo = sb("k2lo", [P, CTOK], F16)
        k2s = sb("k2s", [P, NB, CTOK], F16)
        va2 = sb("va2", [P, GS, H, VW])
        x1 = sb("x1", [P, GS, D])
        x1c = sb("x1c", [P, GS, D])
        st2 = sb("st2", [P, 6])
        mv2 = sb("mv2", [P, 2])
        ve2 = sb("ve2", [P, 1])
        rs2 = sb("rs2", [P, 1])
        xn2 = sb("xn2", [P, GS, D])
        x2t = sb("x2t", [P, L])
        q2hi = sb("q2hi", [P, L], F16)
        q2lo = sb("q2lo", [P, L], F16)
        q2s = sb("q2s", [P, GS, NB, L], F16)
        nm = sb("nm", [P, NJ, NB])
        nmp = sb("nmp", [P, NJ, 32], BF16)
        nmt = sb("nmt", [P, P], BF16)
        prob = sb("prob", [P, NJ, NB * L])
        ots = sb("ots", [P, NJ * L])
        rden = sb("rden", [P, H])
        onorm = sb("onorm", [P, H, HD])
        onormt = sb("onormt", [P, L])
        x2g = sb("x2g", [P, GS, D])
        x2all = sb("x2all", [P, SEQS * D])
        xn3all = sb("xn3all", [P, SEQS * D])
        xn3t = sb("xn3t", [P, TOK])
        pay = sb("pay", [P, GS, TOPK, PAYW])
        lg = sb("lg", [P, GS, E])
        top = sb("top", [P, GS, 8])
        topi = sb("topi", [P, GS, 8], U32)
        topf = sb("topf", [P, GS, TOPK])
        hot = sb("hot", [P, GS, TOPK, E])
        hotb = sb("hotb", [P, GS, E], BF16)
        gap = sb("gap", [P, GS])
        gexp = sb("gexp", [P, GS])
        gden = sb("gden", [P, GS])
        minus1 = sb("minus1", [P, GS])
        seen = sb("seen", [P, E])
        seenb = sb("seenb", [P, E], BF16)
        gsum = sb("gsum", [P, 2, E])
        slot = sb("slot", [P, GS, E])
        picked = sb("picked", [P, GS, TOPK, E])
        destf = sb("destf", [P, GS, TOPK])
        dest = sb("dest", [P, GS, TOPK], I32)

        w1s = sb("w1s", [P, E * HID])
        w2s = sb("w2s", [P, E * HID])
        b1s = sb("b1s", [P, E * HC])
        b2row = sb("b2row", [P, E * D])
        edges = sb("edges", [1, SEQS + NT])
        filler = sb("filler", [P, PAYW])
        counts = sb("counts", [1, E])
        countsi = sb("countsi", [1, E], I32)
        over = sb("over", [1, E, SEQS])
        tiles = sb("tiles", [1, 4, E])
        ones8 = sb("ones8", [1, E])
        isof = sb("isof", [1, 2, NT, E])
        tabf = sb("tabf", [1, 4, NT])
        tab = sb("tab", [1, 4, NT], I32)
        xr = prob[:, :, :].rearrange("p j c -> p (j c)")[:, 0:ROUND * PAYW].rearrange("p (r c) -> p r c", c=PAYW)
        xt = sb("xt", [P, 2, P])
        hs = sb("hs", [P, 2, HID])
        ht = sb("ht", [P, 2, HC, P])
        ys = sb("ys", [P, 2, D])
        yw = sb("yw", [P, 4, D])
        FC = 8
        y2 = [v[:, :, :, :].rearrange("p i h c -> p (i h c)").rearrange("p (k n) -> p k n", k=TOPK) for v in (va, va2)]
        stf = sb("stf", [P, SEQS, 6])
        mvf = sb("mvf", [P, SEQS, 2])
        rsf = sb("rsf", [P, 2, SEQS])
        halff = sb("halff", [P, SEQS])
        gammar = sb("gammar", [P, D])
        betar = sb("betar", [P, D])

        S = [pb(f"S{i}", [P, 512]) for i in range(2)]
        ST = [pb(f"ST{i}", [P, 512]) for i in range(2)]
        AV = pb("AV", [P, 512])
        SM = pb("SM", [P, 512])
        W = [pb(f"W{i}", [P, 512]) for i in range(2)]
        SMb = SM[:, 0:64].bitcast(BF16)

        s_const = sem("s_const")
        s_x = sem("s_x")
        s_ctx = sem("s_ctx")
        s_set = sem("s_set")
        s_cb = sem("s_cb")
        s_xfree = sem("s_xfree")
        s_S = sem("s_S")
        s_max = sem("s_max")
        s_nmp = sem("s_nmp")
        s_sm = sem("s_sm")
        s_smf = sem("s_smf")
        s_st = sem("s_st")
        s_exp = sem("s_exp")
        s_av = sem("s_av")
        s_ot = sem("s_ot")
        s_w = [sem(f"s_w{i}") for i in range(2)]
        s_wf = [sem(f"s_wf{i}") for i in range(2)]
        s_bvb = sem("s_bvb")
        s_cbp = sem("s_cbp")
        s_raw1 = sem("s_raw1")
        s_st1 = sem("s_st1")
        s_nrm1 = sem("s_nrm1")
        s_raw2 = sem("s_raw2")
        s_nrm2 = sem("s_nrm2")
        s_neg = sem("s_neg")
        s_rden = sem("s_rden")
        s_sum = sem("s_sum")
        s_rhi = sem("s_rhi")
        s_route = sem("s_route")
        s_k2hi = sem("s_k2hi")
        s_q2hi = sem("s_q2hi")
        s_xn1 = sem("s_xn1")
        s_rot = sem("s_rot")
        s_parts = sem("s_parts")
        s_x1 = sem("s_x1")
        s_xn2 = sem("s_xn2")
        s_gap = sem("s_gap")
        s_gexp = sem("s_gexp")
        s_keep = sem("s_keep")
        s_pay = sem("s_pay")
        s_rowid = sem("s_rowid")
        s_place = sem("s_place")
        s_seen = sem("s_seen")
        s_copy = sem("s_copy")
        s_x1c = sem("s_x1c")
        s_none = sem("s_none")
        s_hot = sem("s_hot")
        s_scat = sem("s_scat")

        def done(g, t, per=1, c=0):
            return g * (INST * per) + t * per + c + 1

        def sm_count(g, t, what, ended=False):
            c = {"maxima": -2, "sums": 3, "normed": 4, "projected": 5}[what] - (1 if ended else 0)
            if what == "maxima" and is_zero(g, t):
                c = 1
            return g * (INST * 4) + t * 4 + c

        def is_zero(g, t):
            return isinstance(g, int) and g == 0 and t == 0

        def nxt(g, t):
            return (g, t + 1) if t + 1 < INST else (g + 1, 0)

        def prv(g, gp, t):
            return (g, t - 1) if t else (gp, INST - 1)

        def is_first(ph, t):
            return ph.kind == "before" and t == 0

        def is_last(ph, t):
            return ph.kind == "after" and t == INST - 1

        def wait_alone(eng, s, value):
            if not isinstance(value, int):
                eng.compute_val(value)
            eng.wait_ge(s_const, 16 * len(CONSTS))
            eng.wait_ge(s, value)

        def group_of(kind, g, gp):
            return {"next": g + 1, "tail": gp}.get(kind, g)

        def expert_turns(eng, turn):
            for i in range(-2, ROUND + 1):
                turn(0, i, lambda k, i=i: i + k >= 0)
            with eng.Fori(1, NT // ROUND - 1) as m:
                for c in range(1, ROUND + 1):
                    turn(m, c, lambda k: True)
            for c in range(1, ROUND + 1):
                turn(NT // ROUND - 1, c, lambda k, c=c: NT - ROUND + c + k < NT)

        def keys(t):
            return L if t < GS else LC

        def all_steps(eng, step):
            before = Phase("before", 0)
            for t in range(2):
                step(before, 0, None, t)
            with eng.Fori(0, NG - 1) as g:
                body = Phase("body", g)
                for t in range(2, INST):
                    step(body, g, None, t)
                for t in range(2):
                    step(body, g + 1, g, t)
            after = Phase("after", NG - 1)
            for t in range(2, INST):
                step(after, NG - 1, None, t)
            return after

        s_wts = sem("s_wts")
        s_cnt = sem("s_cnt")
        s_cnti = sem("s_cnti")
        s_fill = sem("s_fill")
        s_tabs = sem("s_tabs")
        s_tab = sem("s_tab")
        s_xr = [sem(f"s_xr{i}") for i in range(ROUND)]
        s_xp = sem("s_xp")
        s_xt = sem("s_xt")
        s_h = sem("s_h")
        s_hs = sem("s_hs")
        s_hp = sem("s_hp")
        s_gelu = sem("s_gelu")
        s_y = sem("s_y")
        s_ys = sem("s_ys")
        s_yw = sem("s_yw")
        s_sc = [sem(f"s_sc{i}") for i in range(4)]
        s_xb = sem("s_xb")
        s_y2 = [sem(f"s_y2{i}") for i in range(2)]
        s_add = sem("s_add")
        s_rawf = sem("s_rawf")
        s_stf = sem("s_stf")
        s_rsf = sem("s_rsf")
        s_norm = sem("s_norm")
        s_rsfm = sem("s_rsfm")
        s_gam = sem("s_gam")
        s_fin = sem("s_fin")
        s_out = sem("s_out")

        CONSTS = (
            (wself[:, :, :], w_self), (bself[:, :], b_self), (idf[:, :], ident), (cosb[:, :], cos_t),
            (sinb[:, :], sin_t), (selq[:, :, :, :], sel_q), (selk[:, :, :, :], sel_k),
            (idb[:, :], ident_bf), (onesr[:, :, :, :], ones_rows), (wcross[:, :, :], w_cross),
            (bcross[:, :], b_cross), (upperb[:, :], upper), (etab[:, :, :], ebase), (wgs[:, :], wg),
            (rowid[:, :, :], row_id), (bprow[:, :], bp.partition_broadcast(P)),
            (borow[:, :], bo.partition_broadcast(P)), (bgrow[:, :], bg.partition_broadcast(P)),
            (b1s[:, :], b1),
            (b2row[:, :], b2.rearrange("e d -> (e d)").partition_broadcast(P)),
            (gammar[:, :], gamma.partition_broadcast(P)), (betar[:, :], beta.partition_broadcast(P)),
        )
        SET_STEPS = 10

        block = stack.enter_context(nc.Block())


        @block.sync
        def _(sp):
            sp.dma_start(xin[:, :, :], x_rows[:, 0, :, :]).then_inc(s_x, 16)
            for dst, src in CONSTS:
                sp.dma_start(dst, src).then_inc(s_const, 16)
            sp.dma_start(ctxb[:, :], ctx_t[:, 0:CTOK]).then_inc(s_ctx, 16)
            sp.dma_start(edges[:, :], tile_edge).then_inc(s_keep, 16)
            for e in range(E):
                at = slice(e * HID, (e + 1) * HID)
                sp.dma_start(w1s[:, at], w1[e, :, :]).then_inc(s_wts, 16)
                sp.dma_start(w2s[:, at].rearrange("p (c d) -> p c d", d=D),
                             w2[e, :, :].rearrange("(c p) d -> p c d", p=P)).then_inc(s_wts, 16)

            def keep(g):
                sp.wait_ge(s_xn2, done(g, INST - 1))
                at = bass.ds(g * (GS * D), GS * D)
                sp.dma_start(x2all[:, at], x2g[:, :, :].rearrange("p i d -> p (i d)")).then_inc(s_keep, 16)
                sp.dma_start(xn3all[:, at].rearrange("p (i d) -> p i d", d=D), pay[:, :, 0, 0:D]).then_inc(s_keep, 16)

            with sp.Fori(0, NG - 1) as g:
                sp.wait_ge(s_xfree, g + 1)
                sp.dma_start(xin[:, :, :], x_rows[:, bass.ds(g + 1, 1), :, :].rearrange("l a i d -> l (a i) d")).then_inc(s_x, 16)
                sp.wait_ge(s_q2hi, g * GS + 1)
                sp.dma_start(ctxb[:, :], ctx_t[:, bass.ds((g + 1) * CTOK, CTOK)]).then_inc(s_ctx, 16)
                keep(g)
            keep(NG - 1)
            sp.wait_ge(s_scat, 16)
            sp.dma_start(routed[SPARE:SPARE + P, :], filler[:, :]).then_inc(s_fill, 16)
            sp.wait_ge(s_cnti, 1)
            for e in range(E):
                c = sp.value_load(countsi[0:1, e:e + 1], min_val=0, max_val=NTOK)
                sp.dma_start(routed[bass.ds(c + e * REGION, P), :], filler[:, :]).then_inc(s_fill, 16)
            sp.wait_ge(s_fill, 16 * (E + 1))
            sp.wait_ge(s_scat, 16 * (NG + 1) * GS * TOPK + 16)
            sp.wait_ge(s_tab, 1)

            def load(m, c):
                row = sp.value_load(tab[0:1, 1, bass.ds(m * ROUND + c, 1)], min_val=0, max_val=SPARE)
                sp.dma_start(xr[:, c, :], routed[bass.ds(row, P), :]).then_inc(s_xr[c], 16)

            for c in range(ROUND):
                load(0, c)
            with sp.Fori(1, NT // ROUND) as m:
                for c in range(ROUND):
                    sp.wait_ge(s_sc[c % 4], m * 32 - 16 + 16 * (c // 4))
                    load(m, c)
            for k in range(4):
                sp.wait_ge(s_sc[k], 16 * NT // 4)
            for n in range(SEQS // FC):
                if n >= 2:
                    sp.wait_ge(s_add, 2 * (n - 1))
                for k in range(TOPK):
                    r0 = k * NTOK + n * FC * L
                    sp.dma_start(y2[n % 2][:, k, :].rearrange("p (s d) -> p s d", d=D),
                                 expert_out[r0:r0 + FC * L, :].rearrange("(s p) d -> p s d", p=P)).then_inc(s_y2[n % 2], 16)
            for n in range(SEQS // FC):
                sp.wait_ge(s_fin, n + 1)
                sp.dma_start(out_rows[:, n * FC:(n + 1) * FC, :],
                             x2all[:, n * FC * D:(n + 1) * FC * D].rearrange("p (s d) -> p s d", d=D)).then_inc(s_out, 16)
            sp.wait_ge(s_out, 16 * (SEQS // FC))

        @block.tensor
        def _(pe):
            mm = nc.tensor.matmul
            tr = nc.tensor.transpose
            pe.wait_ge(s_const, 16 * len(CONSTS))
            pe.wait_ge(s_set, SET_STEPS)
            pe.wait_ge(s_bvb, 2)
            mm(S[0][:, 0:D], bvb[:, 0, :], wself[:, 5, :], start=True, stop=True).then_inc(s_cbp, 1)
            mm(S[1][:, 0:D], bvb[:, 1, :], wcross[:, 3, :], start=True, stop=True).then_inc(s_cbp, 1)
            pe.wait_ge(s_cb, 2)

            def scores(ph, g, t, j):
                first = is_zero(g, t)
                u = done(g, t, NJ, j)
                if j == 0 and t == 0:
                    for name in ("gk3", "gk1"):
                        bank, c = ph.item(name)
                        pe.wait_ge(s_wf[bank], c)
                if j == 0 and t >= GS:
                    bank, c = ph.item(f"gq2{t - GS}")
                    pe.wait_ge(s_wf[bank], c)
                if not (first and j < 2):
                    pe.wait_ge(s_max, u - 2)
                bank = S[j % 2]
                n = keys(t)
                rows = slice(32 * j, 32 * j + 32)
                for b in range(NB):
                    if t < GS:
                        q, k = qs[rows, b, t * L:(t + 1) * L], ks[rows, b, t * L:(t + 1) * L]
                    else:
                        i = t - GS
                        q, k = q2s[rows, i, b, :], k2s[rows, b, i * LC:(i + 1) * LC]
                    last = mm(bank[:, b * n:(b + 1) * n], q, k, start=True, stop=True)
                last.then_inc(s_S, 1)

            def shifted(ph, g, t, j):
                first = is_zero(g, t)
                if j == 0:
                    pe.wait_ge(s_smf, sm_count(g, t, "maxima"))
                if not (first and j < 2):
                    pe.wait_ge(s_exp, done(g, t, NJ, j) - 2)
                n = keys(t)
                rows = slice(32 * j, 32 * j + 32)
                for b in range(NB):
                    o = ST[j % 2][0:n, b * L:(b + 1) * L]
                    if t < GS:
                        q, k = qs[rows, b, t * L:(t + 1) * L], ks[rows, b, t * L:(t + 1) * L]
                    else:
                        i = t - GS
                        q, k = q2s[rows, i, b, :], k2s[rows, b, i * LC:(i + 1) * LC]
                    mm(o, onesr[:, j, b, 0:n], nmt[:, :], start=True, stop=False)
                    last = mm(o, k, q, start=False, stop=True)
                last.then_inc(s_st, 1)

            def values(ph, g, t, j):
                if j == 0 and not is_first(ph, t):
                    pe.wait_ge(s_ot, done(g, t) - 1)
                pe.wait_ge(s_exp, done(g, t, NJ, j))
                n = keys(t)
                v = va if t < GS else va2
                for b in range(NB):
                    last = mm(AV[32 * b:32 * b + 32, j * L:(j + 1) * L], v[0:n, t % GS, NB * j + b, :],
                              prob[0:n, j, b * L:(b + 1) * L], start=True, stop=True)
                last.then_inc(s_av, 1)

            def small(what, g, t, ended=False):
                c = sm_count(g, t, what, ended)
                if not (is_zero(g, t) and what == "maxima"):
                    pe.wait_ge(s_smf, c - 1)
                if what == "maxima":
                    pe.wait_ge(s_nmp, done(g, t))
                    tr(SMb, nmp[:, :, :].rearrange("p j c -> p (j c)"), idb[:, :]).then_inc(s_sm, 1)
                elif what == "sums":
                    pe.wait_ge(s_ot, done(g, t))
                    for j in range(NJ):
                        last = tr(SM[:, j * L:(j + 1) * L], ots[:, j * L:(j + 1) * L], idf[:, :])
                    last.then_inc(s_sm, 1)
                elif what == "normed":
                    tr(SM[:, 0:L], onorm[:, :, :].rearrange("p h c -> p (h c)"), idf[:, :]).then_inc(s_sm, 1)
                else:
                    w = wself[:, 5, :] if t < GS else wcross[:, 3, :]
                    mm(SM[:, 0:D], onormt[:, :], w, start=True, stop=True).then_inc(s_sm, 1)

            def work(ph, g, name):
                bank, c = ph.item(name)
                w = W[bank]
                if not (ph.kind == "before" and c == 1):
                    pe.wait_ge(s_wf[bank], c - 1)
                if name == "xnt":
                    pe.wait_ge(s_xn1, g * GS + GS)
                    for i in range(GS):
                        last = tr(w[:, i * L:(i + 1) * L], xn1[:, i, :], idf[:, :])
                elif name in ("q", "rq", "k", "rk"):
                    fb, fc = ph.item("xnt")
                    pe.wait_ge(s_wf[fb], fc)
                    last = mm(w[:, :], wself[:, ("q", "rq", "k", "rk").index(name), :], xnt[:, :], start=True, stop=True)
                elif name == "v":
                    for i in range(GS):
                        last = mm(w[:, i * D:(i + 1) * D], xnt[:, i * L:(i + 1) * L], wself[:, 4, :], start=True, stop=True)
                elif name[:2] in ("gq", "gk") and name[2] != "2" or name in ("gq2", "gk2"):
                    b, k = int(name[2]), 0 if name[1] == "q" else 1
                    sel = selq if k == 0 else selk
                    pe.wait_ge(s_parts, g * 2 + k + 1)
                    mm(w[:, :], sel[:, 0, b, :], rhi[:, k, :], start=True, stop=False)
                    last = mm(w[:, :], sel[:, 1, b, :], rlo[:, k, :], start=False, stop=True)
                elif name == "k2":
                    pe.wait_ge(s_ctx, g * 16 + 16)
                    last = mm(w[:, 0:CTOK], wcross[:, 1, :], ctxb[:, :], start=True, stop=True)
                elif name == "v2":
                    for i in range(GS):
                        last = mm(w[0:LC, i * D:(i + 1) * D], ctxb[:, i * LC:(i + 1) * LC], wcross[:, 2, :],
                                  start=True, stop=True)
                elif name.startswith("gk2"):
                    b = int(name[3])
                    fb, fc = ph.item("k2")
                    pe.wait_ge(s_wf[fb], fc)
                    mm(w[:, 0:CTOK], selk[:, 0, b, :], k2hi[:, :], start=True, stop=False)
                    last = mm(w[:, 0:CTOK], selk[:, 1, b, :], k2lo[:, :], start=False, stop=True)
                elif name.startswith("x2t"):
                    i = int(name[3])
                    pe.wait_ge(s_xn2, done(g, i))
                    last = tr(w[:, 0:L], xn2[:, i, :], idf[:, :])
                elif name.startswith("q2"):
                    fb, fc = ph.item("x2t" + name[2])
                    pe.wait_ge(s_wf[fb], fc)
                    last = mm(w[:, 0:L], wcross[:, 0, :], x2t[:, :], start=True, stop=True)
                elif name.startswith("gq2"):
                    fb, fc = ph.item("q2" + name[3])
                    pe.wait_ge(s_wf[fb], fc)
                    for b in range(NB):
                        o = w[:, b * L:(b + 1) * L]
                        mm(o, selq[:, 0, b, :], q2hi[:, :], start=True, stop=False)
                        last = mm(o, selq[:, 1, b, :], q2lo[:, :], start=False, stop=True)
                elif name.startswith("x3t"):
                    i = int(name[3])
                    pe.wait_ge(s_xn2, done(g, GS + i))
                    last = tr(w[:, 0:L], pay[:, i, 0, 0:D], idf[:, :])
                elif name == "log":
                    fb, fc = ph.item("x3t3")
                    pe.wait_ge(s_wf[fb], fc)
                    for i in range(GS):
                        last = mm(w[:, i * E:(i + 1) * E], xn3t[:, i * L:(i + 1) * L], wgs[:, :], start=True, stop=True)
                else:
                    pe.wait_ge(s_hot, g + 1)
                    wait_alone(pe, s_seen, g + 1)
                    hb = hotb[:, :, :]
                    mm(w[:, 0:GS * E], upperb[:, :], hb.rearrange("p i e -> p (i e)"), start=True, stop=False)
                    for i in range(1, GS):
                        mm(w[:, i * E:GS * E], onesb[:, :], hb[:, 0:GS - i, :].rearrange("p i e -> p (i e)"),
                           start=False, stop=False)
                    for i in range(GS):
                        last = mm(w[:, i * E:(i + 1) * E], onesb[:, :], seenb[:, :], start=False, stop=(i == GS - 1))
                last.then_inc(s_w[bank], 1)

            def step(ph, g, gp, t):
                for j in range(NJ):
                    if not is_last(ph, t):
                        scores(ph, *nxt(g, t), j)
                    shifted(ph, g, t, j)
                    if j:
                        values(ph, g, t, j - 1)
                    if not is_first(ph, t) and j < 3:
                        small(("sums", "normed", "projected")[j], *prv(g, gp, t))
                    for name, kind in ph.at(t, j):
                        work(ph, group_of(kind, g, gp), name)
                values(ph, g, t, NJ - 1)
                if not is_last(ph, t):
                    small("maxima", *nxt(g, t))

            before = Phase("before", 0)
            for name, _ in NEXT_ITEMS:
                work(before, 0, name)
            for j in range(NJ):
                scores(before, 0, 0, j)
            small("maxima", 0, 0)
            after = all_steps(pe, step)
            for k in ("sums", "normed", "projected"):
                small(k, NG - 1, INST - 1, ended=True)
            for name, _ in TAIL_ITEMS:
                work(after, NG - 1, name)


            pe.wait_ge(s_pay, NG + 1)
            pe.wait_ge(s_max, NG * INST * NJ)
            mm(S[0][:, 0:E], onesb[:, :], seenb[:, :], start=True, stop=True).then_inc(s_cnt, 1)
            pe.wait_ge(s_tab, 1)
            pe.wait_ge(s_wts, 16 * 2 * E)

            def expert_of(n):
                return pe.value_load(tab[0:1, 0, bass.ds(n, 1)], min_val=0, max_val=(E - 1) * HID)

            def turn(m, c, has):
                e1 = expert_of(m * ROUND + c + 1) if has(1) else None
                e2 = expert_of(m * ROUND + c - 1) if has(-1) else None
                if has(0):
                    n, k = m * ROUND + c, c % 2
                    pe.wait_ge(s_hs, n + 1)
                    if has(-2):
                        pe.wait_ge(s_gelu, n - 1)
                    for q in range(HC):
                        last = tr(ST[k][:, q * P:(q + 1) * P], hs[:, k, q * P:(q + 1) * P], idf[:, :])
                    last.then_inc(s_hp, 1)
                if has(2):
                    n, k, r = m * ROUND + c + 2, (c + 2) % 2, (c + 2) % ROUND
                    pe.wait_ge(s_xr[r], (m + (c + 2) // ROUND) * 16 + 16)
                    if has(0):
                        pe.wait_ge(s_xt, n - 1)
                    tr(W[k][:, 0:P], xr[:, r, 0:D], idf[:, :]).then_inc(s_xp, 1)
                if has(1):
                    n, k = m * ROUND + c + 1, (c + 1) % 2
                    pe.wait_ge(s_xt, n + 1)
                    if has(-1):
                        pe.wait_ge(s_hs, n - 1)
                    mm(S[k][:, :], xt[:, k, :], w1s[:, bass.ds(e1, HID)], start=True, stop=True).then_inc(s_h, 1)
                if has(-1):
                    n, k = m * ROUND + c - 1, (c - 1) % 2
                    pe.wait_ge(s_gelu, n + 1)
                    if has(-3):
                        pe.wait_ge(s_ys, n - 1)
                    for q in range(HC):
                        last = mm((AV, SM)[k][:, 0:D], ht[:, k, q, :], w2s[:, bass.ds(e2 + q * D, D)],
                                  start=(q == 0), stop=(q == HC - 1))
                    last.then_inc(s_y, 1)

            expert_turns(pe, turn)

        @block.scalar
        def _(act):
            act.wait_ge(s_const, 16 * len(CONSTS))
            act.wait_ge(s_set, SET_STEPS)

            def move(dst, src, s, **kw):
                act.activation(dst, src, ACT.Copy).then_inc(s, 1)

            def exps(g, t, j):
                act.wait_ge(s_st, done(g, t, NJ, j))
                if not is_zero(g, t):
                    act.wait_ge(s_av, done(g, t, NJ, j) - NJ)
                n = keys(t)
                act.activation(prob[0:n, j, :], ST[j % 2][0:n, :], ACT.Exp, scale=SCALE).then_inc(s_exp, 1)

            def small(what, g, t, ended=False):
                act.wait_ge(s_sm, sm_count(g, t, what, ended))
                if what == "maxima":
                    move(nmt[:, :], SMb, s_smf)
                else:
                    move(onormt[:, :], SM[:, 0:L], s_smf)

            def sums_out(g, t):
                act.wait_ge(s_av, done(g, t, NJ, NJ - 1))
                move(ots[:, :], AV[:, :], s_ot)

            def high_part(g, k):
                act.wait_ge(s_sum, g * 2 + k + 1)
                act.activation(rhi[:, k, :], rsum[:, k, :], ACT.Copy).then_inc(s_rhi, 1)

            def work(ph, g, name):
                bank, c = ph.item(name)
                w = W[bank]
                if name in ("q", "rq", "k", "rk", "gk0", "gk1", "gk2", "gk3", "log", "pos"):
                    return
                act.wait_ge(s_w[bank], c)
                if name == "xnt":
                    move(xnt[:, :], w[:, :], s_wf[bank])
                elif name == "v":
                    move(va[:, :, :, 0:HD].rearrange("p i h c -> p (i h) c"),
                         w[:, :].rearrange("p (n c) -> p n c", c=HD), s_wf[bank])
                elif name in ("gq0", "gq1", "gq2", "gq3"):
                    move(qs[:, int(name[2]), :], w[:, :], s_wf[bank])
                elif name == "k2":
                    act.activation(k2hi[:, :], w[:, 0:CTOK], ACT.Identity, bias=bcross[:, 1:2]).then_inc(s_k2hi, 1)
                elif name == "v2":
                    act.activation(va2[0:LC, :, :, 0:HD].rearrange("p i h c -> p (i h) c"),
                                   w[0:LC, :].rearrange("p (n c) -> p n c", c=HD), ACT.Copy).then_inc(s_wf[bank], 1)
                elif name.startswith("gk2"):
                    move(k2s[:, int(name[3]), :], w[:, 0:CTOK], s_wf[bank])
                elif name.startswith("x2t"):
                    move(x2t[:, :], w[:, 0:L], s_wf[bank])
                elif name.startswith("q2"):
                    act.activation(q2hi[:, :], w[:, 0:L], ACT.Identity, bias=bcross[:, 0:1]).then_inc(s_q2hi, 1)
                elif name.startswith("gq2"):
                    move(q2s[:, int(name[3]), :, :].rearrange("p b l -> p (b l)"), w[:, :], s_wf[bank])
                elif name.startswith("x3t"):
                    i = int(name[3])
                    act.activation(pay[:, i, 1, 0:D], pay[:, i, 0, 0:D], ACT.Copy).then_inc(s_copy, 1)
                    move(xn3t[:, i * L:(i + 1) * L], w[:, 0:L], s_wf[bank])

            def step(ph, g, gp, t):
                if not is_first(ph, t):
                    sums_out(*prv(g, gp, t))
                for j in range(NJ):
                    exps(g, t, j)
                    if j == 1 and not is_first(ph, t):
                        small("normed", *prv(g, gp, t))
                    if ph.kind == "body" and (t, j) in ((3, 3), (4, 2)):
                        high_part(g + 1, t - 3)
                    if j == 3 and t == 1 and gp is not None:
                        act.wait_ge(s_gap, gp + 1)
                        act.activation(gexp[:, :], gap[:, :], ACT.Exp).then_inc(s_gexp, 1)
                    for name, kind in ph.at(t, j):
                        work(ph, group_of(kind, g, gp), name)
                if not is_last(ph, t):
                    small("maxima", *nxt(g, t))

            before = Phase("before", 0)
            for name, _ in NEXT_ITEMS:
                work(before, 0, name)
                if name in ("rq", "rk"):
                    high_part(0, ("rq", "rk").index(name))
            small("maxima", 0, 0)
            after = all_steps(act, step)
            sums_out(NG - 1, INST - 1)
            small("normed", NG - 1, INST - 1, ended=True)
            for name, _ in TAIL_ITEMS:
                work(after, NG - 1, name)
            act.wait_ge(s_gap, NG)
            act.activation(gexp[:, :], gap[:, :], ACT.Exp).then_inc(s_gexp, 1)
            act.wait_ge(s_tab, 1)

            def turn(m, c, has):
                if has(0):
                    n, k = m * ROUND + c, c % 2
                    b = act.value_load(tab[0:1, 2, bass.ds(n, 1)], min_val=0, max_val=(E - 1) * HC)
                    act.wait_ge(s_hp, n + 1)
                    if has(-2):
                        act.wait_ge(s_y, n - 1)
                    for q in range(HC):
                        last = act.activation(ht[:, k, q, :], ST[k][:, q * P:(q + 1) * P], ACT.Gelu,
                                              bias=b1s[:, bass.ds(b + q, 1)])
                    last.then_inc(s_gelu, 1)

            expert_turns(act, turn)

            for i in range(SEQS):
                if i % FC == 0:
                    act.wait_ge(s_rsf, 3 * (i // FC + 1))
                act.activation(xn3all[:, i * D:(i + 1) * D], xn3all[:, i * D:(i + 1) * D], ACT.Identity,
                               bias=rsf[:, 1, i:i + 1], scale=rsf[:, 0, i:i + 1]).then_inc(s_norm, 1)

        @block.vector
        def _(dve):
            V = nc.vector
            dve.wait_ge(s_const, 16 * len(CONSTS))
            dve.wait_ge(s_set, SET_STEPS)
            V.tensor_scalar(bvb[:, 0, :], idf[:, :], 0.0, bself[:, 4:5], ALU.mult, ALU.add).then_inc(s_bvb, 1)
            V.tensor_scalar(bvb[:, 1, :], idf[:, :], 0.0, bcross[:, 2:3], ALU.mult, ALU.add).then_inc(s_bvb, 1)
            dve.wait_ge(s_cbp, 2)
            V.tensor_tensor(cself[:, :], S[0][:, 0:D], bprow[:, :], ALU.add).then_inc(s_cb, 1)
            V.tensor_tensor(ccross[:, :], S[1][:, 0:D], borow[:, :], ALU.add).then_inc(s_cb, 1)

            def statistics(g):
                wait_alone(dve, s_x, g * 16 + 16)
                for i in range(GS):
                    V.bn_stats(st1[:, i, :], xin[:, i, :]).then_inc(s_raw1, 1)
                wait_alone(dve, s_raw1, g * GS + GS)
                for i in range(GS):
                    V.bn_aggr(mv1[:, i, :], st1[:, i, :]).then_inc(s_st1, 1)

            def normed_group(g):
                wait_alone(dve, s_nrm1, g * 2 + 2)
                for i in range(GS):
                    V.tensor_scalar(xn1[:, i, :], xin[:, i, :], mv1[:, i, 0:1], rs1[:, i:i + 1],
                                    ALU.subtract, ALU.mult).then_inc(s_xn1, 1)

            def maxima(g, t, j):
                n = keys(t)
                dve.wait_ge(s_S, done(g, t, NJ, j))
                V.tensor_reduce(nm[:, j, :], S[j % 2][:, 0:NB * n].rearrange("p (b k) -> p b k", b=NB),
                                AX.X, ALU.max, negate=True).then_inc(s_max, 1)

            def maxima_parts(g, t, last=None):
                dve.wait_ge(s_max, done(g, t, NJ, NJ - 1))
                if last:
                    dve.wait_ge(s_sm, sm_count(*last, "maxima"))
                V.tensor_copy(nmp[:, :, 0:NB], nm[:, :, :]).then_inc(s_neg, 1)
                dve.wait_ge(s_neg, done(g, t))
                V.tensor_tensor(nmp[:, :, NB:2 * NB], nm[:, :, :], nmp[:, :, 0:NB], ALU.subtract).then_inc(s_nmp, 1)

            def norm_rows(g, t, ended=False):
                dve.wait_ge(s_sm, sm_count(g, t, "sums", ended))
                o = SM[:, :].rearrange("p (h c) -> p h c", c=VW)
                V.reciprocal(rden[:, :], o[:, :, HD:HD + 1].rearrange("p h c -> p (h c)")).then_inc(s_rden, 1)
                dve.wait_ge(s_rden, done(g, t))
                V.tensor_tensor(onorm[:, :, :], o[:, :, 0:HD],
                                rden[:, :].unsqueeze(2).to_broadcast([P, H, HD]), ALU.mult).then_inc(s_smf, 1)

            def residual(g, t, ended=False):
                dve.wait_ge(s_sm, sm_count(g, t, "projected", ended))
                i = t % GS
                if t < GS:
                    dve.wait_ge(s_xfree, g + 1)
                    row, more = x1[:, i, :], xc[:, i, :]
                else:
                    if t == GS:
                        dve.wait_ge(s_keep, g * 32 + 16)
                    dve.wait_ge(s_x1c, g * GS + i + 1)
                    row, more = x2g[:, i, :], x1c[:, i, :]
                V.tensor_tensor(row, SM[:, 0:D], more, ALU.add).then_inc(s_smf, 1)

            def residual_statistics(g, t, ended=False):
                i = t % GS
                row = x1[:, i, :] if t < GS else x2g[:, i, :]
                wait_alone(dve, s_smf, sm_count(g, t, "projected", ended))
                V.bn_stats(st2[:, :], row).then_inc(s_raw2, 1)
                if not is_zero(g, t):
                    wait_alone(dve, s_xn2, done(g, t) - 1)
                wait_alone(dve, s_raw2, done(g, t))
                V.bn_aggr(mv2[:, :], st2[:, :]).then_inc(s_x1, 1)

            def work(ph, g, name):
                bank, c = ph.item(name)
                w = W[bank]
                w3 = w[:, :].rearrange("p (i l) -> p i l", i=GS)
                if name in ("q", "rq", "k", "rk"):
                    n = ("q", "rq", "k", "rk").index(name)
                    table, to = (sinb, rb) if n % 2 else (cosb, ra)
                    dve.wait_ge(s_w[bank], c)
                    V.scalar_tensor_tensor(
                        to[:, n // 2, :].rearrange("p (i l) -> p i l", i=GS), w3, bself[:, n:n + 1],
                        table[:, :].unsqueeze(1).to_broadcast([P, GS, L]), ALU.add, ALU.mult).then_inc(s_wf[bank], 1)
                    if n % 2:
                        for half_item in (("q", "rq"), ("k", "rk"))[n // 2]:
                            fb, fc = ph.item(half_item)
                            dve.wait_ge(s_wf[fb], fc)
                        V.tensor_tensor(rsum[:, n // 2, :], ra[:, n // 2, :], rb[:, n // 2, :], ALU.add).then_inc(s_sum, 1)
                elif name in ("gk0", "gk1", "gk2", "gk3"):
                    dve.wait_ge(s_w[bank], c)
                    V.tensor_copy(ks[:, int(name[2]), :], w[:, :]).then_inc(s_wf[bank], 1)
                elif name == "k2":
                    dve.wait_ge(s_k2hi, g + 1)
                    V.scalar_tensor_tensor(k2lo[:, :], w[:, 0:CTOK], bcross[:, 1:2], k2hi[:, :],
                                           ALU.add, ALU.subtract).then_inc(s_wf[bank], 1)
                elif name in ("q20", "q21", "q22", "q23"):
                    dve.wait_ge(s_q2hi, g * GS + int(name[2]) + 1)
                    V.scalar_tensor_tensor(q2lo[:, :], w[:, 0:L], bcross[:, 0:1], q2hi[:, :],
                                           ALU.add, ALU.subtract).then_inc(s_wf[bank], 1)
                elif name == "log":
                    choose(g, w, bank, c)
                elif name == "pos":
                    place(g, w, bank, c)

            CHOOSE = 2 * GS + 2

            def routed_step(g, n, ins, alone=False, wait=True):
                ins.then_inc(s_route, 1)
                if wait and alone:
                    wait_alone(dve, s_route, g * CHOOSE + n)
                elif wait:
                    dve.wait_ge(s_route, g * CHOOSE + n)

            def choose(g, w, bank, c):
                dve.wait_ge(s_w[bank], c)
                V.tensor_tensor(lg[:, :, :], w[:, 0:GS * E].rearrange("p (i e) -> p i e", e=E),
                                bgrow[:, :].unsqueeze(1).to_broadcast([P, GS, E]), ALU.add).then_inc(s_wf[bank], 1)
                wait_alone(dve, s_wf[bank], c)
                for i in range(GS):
                    routed_step(g, i + 1, V.max(top[:, i, :], lg[:, i, :]), alone=True, wait=(i == GS - 1))
                for i in range(GS):
                    routed_step(g, GS + i + 1, V.max_index(topi[:, i, :], top[:, i, :], lg[:, i, :]), wait=False)

            def mark(g):
                n = 2 * GS
                dve.wait_ge(s_route, g * CHOOSE + n)
                routed_step(g, n + 1, V.tensor_copy(topf[:, :, :], topi[:, :, 0:TOPK]))
                routed_step(g, n + 2, V.tensor_tensor(
                    hot[:, :, :, :], iota8.unsqueeze(1).unsqueeze(1).to_broadcast([P, GS, TOPK, E]),
                    topf[:, :, :].unsqueeze(3).to_broadcast([P, GS, TOPK, E]), ALU.is_equal))
                V.tensor_tensor(hotb[:, :, :], hot[:, :, 0, :], hot[:, :, 1, :], ALU.add).then_inc(s_hot, 1)
                V.tensor_tensor(gap[:, :], top[:, :, 1], top[:, :, 0], ALU.subtract).then_inc(s_gap, 1)

            def place(g, w, bank, c):
                dve.wait_ge(s_w[bank], c)
                V.tensor_tensor(slot[:, :, :], w[:, 0:GS * E].rearrange("p (i e) -> p i e", e=E),
                                ebaser.unsqueeze(1).to_broadcast([P, GS, E]), ALU.add).then_inc(s_wf[bank], 1)
                V.tensor_copy(pay[:, :, :, D + 1].bitcast(I32), rowid[:, bass.ds(g * GS, GS), :]).then_inc(s_rowid, 1)

            EARLY = (0,)

            def step(ph, g, gp, t):
                for j in range(NJ):
                    if not is_first(ph, t) and j == 3:
                        residual(*prv(g, gp, t))
                        if t in EARLY:
                            residual_statistics(*prv(g, gp, t))
                    if not is_last(ph, t):
                        maxima(*nxt(g, t), j)
                    if t == 1 and j == 2 and gp is not None:
                        mark(gp)
                    if t == 2 and j == 1 and ph.kind == "body":
                        statistics(g + 1)
                    if not is_first(ph, t) and j == 0:
                        norm_rows(*prv(g, gp, t))
                    if j == NJ - 1 and not is_last(ph, t):
                        maxima_parts(*nxt(g, t), last=(g, t))
                    if j == 3 and not is_first(ph, t) and t not in EARLY:
                        residual_statistics(*prv(g, gp, t))
                    if t == 2 and j == 3 and ph.kind == "body":
                        normed_group(g + 1)
                    for name, kind in ph.at(t, j):
                        work(ph, group_of(kind, g, gp), name)

            before = Phase("before", 0)
            statistics(0)
            normed_group(0)
            for name, _ in NEXT_ITEMS:
                work(before, 0, name)
            for j in range(NJ):
                maxima(0, 0, j)
            maxima_parts(0, 0)
            after = all_steps(dve, step)
            norm_rows(NG - 1, INST - 1, ended=True)
            residual(NG - 1, INST - 1, ended=True)
            residual_statistics(NG - 1, INST - 1, ended=True)
            for name, _ in TAIL_ITEMS:
                if name == "pos":
                    mark(NG - 1)
                work(after, NG - 1, name)

            nt = 0

            def did(ins):
                nonlocal nt
                ins.then_inc(s_tabs, 1)
                nt += 1
                dve.wait_ge(s_tabs, nt)

            dve.wait_ge(s_cnt, 1)
            did(V.tensor_copy(counts[:, :], S[0][0:1, 0:E]))
            V.tensor_copy(countsi[:, :], counts[:, :]).then_inc(s_cnti, 1)
            did(V.memset(ones8[:, :], 1.0))
            did(V.tensor_tensor(over[:, :, :], counts[:, :].unsqueeze(2).to_broadcast([1, E, SEQS]),
                                edges[:, 0:SEQS].unsqueeze(1).to_broadcast([1, E, SEQS]), ALU.is_gt))
            did(V.tensor_reduce(tiles[:, 0, :], over[:, :, :], AX.X, ALU.add))
            did(V.tensor_tensor_scan(tiles[:, 1, :], ones8[:, :], tiles[:, 0, :], 0.0, ALU.mult, ALU.add))
            did(V.tensor_tensor(tiles[:, 2, :], tiles[:, 1, :], tiles[:, 0, :], ALU.subtract))
            did(V.scalar_tensor_tensor(tiles[:, 3, :], tiles[:, 2, :], -float(P), etab[0:1, 0, :], ALU.mult, ALU.add))
            number = edges[:, SEQS:SEQS + NT].unsqueeze(2).to_broadcast([1, NT, E])
            for k in range(2):
                did(V.tensor_tensor(isof[:, k, :, :], number,
                                    tiles[:, 2 - k, :].unsqueeze(1).to_broadcast([1, NT, E]), ALU.is_ge))
            did(V.tensor_tensor(isof[:, 0, :, :], isof[:, 0, :, :], isof[:, 1, :, :], ALU.subtract))
            did(V.tensor_reduce(tabf[:, 3, :], isof[:, 0, :, :], AX.X, ALU.add))
            did(V.tensor_tensor(isof[:, 1, :, :], isof[:, 0, :, :],
                                tiles[:, 3, :].unsqueeze(1).to_broadcast([1, NT, E]), ALU.mult))
            did(V.tensor_reduce(tabf[:, 1, :], isof[:, 1, :, :], AX.X, ALU.add))
            did(V.tensor_tensor(isof[:, 1, :, :], isof[:, 0, :, :],
                                etab[0:1, 1, :].unsqueeze(1).to_broadcast([1, NT, E]), ALU.mult))
            did(V.tensor_reduce(tabf[:, 2, :], isof[:, 1, :, :], AX.X, ALU.add))
            did(V.tensor_scalar(tabf[:, 0, :], edges[:, SEQS:SEQS + NT], float(P), -float(SPARE), ALU.mult, ALU.add))
            did(V.tensor_tensor(tabf[:, 0, :], tabf[:, 0, :], tabf[:, 3, :], ALU.mult))
            did(V.tensor_tensor(tabf[:, 0, :], tabf[:, 0, :], tabf[:, 1, :], ALU.add))
            did(V.tensor_scalar(tabf[:, 1, :], tabf[:, 0, :], float(SPARE), None, ALU.add))
            did(V.tensor_scalar(tabf[:, 0, :], tabf[:, 2, :], float(HID), None, ALU.mult))
            did(V.tensor_scalar(tabf[:, 3, :], tabf[:, 2, :], float(D), None, ALU.mult))
            did(V.tensor_scalar(tabf[:, 2, :], tabf[:, 2, :], float(HC), None, ALU.mult))
            V.tensor_copy(tab[:, :, :], tabf[:, :, :]).then_inc(s_tab, 1)
            dve.wait_ge(s_tab, 1)

            def turn(m, c, has):
                if has(2):
                    n, k = m * ROUND + c + 2, (c + 2) % 2
                    dve.wait_ge(s_xp, n + 1)
                    if has(0):
                        dve.wait_ge(s_h, n - 1)
                    V.tensor_copy(xt[:, k, :], W[k][:, 0:P]).then_inc(s_xt, 1)
                if has(1):
                    n, k = m * ROUND + c + 1, (c + 1) % 2
                    dve.wait_ge(s_h, n + 1)
                    if has(-1):
                        dve.wait_ge(s_hp, n - 1)
                    V.tensor_copy(hs[:, k, :], S[k][:, :]).then_inc(s_hs, 1)
                if has(-1):
                    n, k = m * ROUND + c - 1, (c - 1) % 2
                    e = dve.value_load(tab[0:1, 3, bass.ds(n, 1)], min_val=0, max_val=(E - 1) * D)
                    dve.wait_ge(s_y, n + 1)
                    if has(-3):
                        dve.wait_ge(s_yw, n - 1)
                    V.tensor_tensor(ys[:, k, :], (AV, SM)[k][:, 0:D], b2row[:, bass.ds(e, D)], ALU.add).then_inc(s_ys, 1)

            expert_turns(dve, turn)

            def chunk_sums(n):
                at = slice(n * FC * D, (n + 1) * FC * D)
                dve.wait_ge(s_y2[n % 2], 16 * TOPK * (n // 2 + 1))
                for k in range(TOPK):
                    V.tensor_tensor(xn3all[:, at], xn3all[:, at], y2[n % 2][:, k, :], ALU.add).then_inc(s_add, 1)
                    dve.wait_ge(s_add, TOPK * n + k + 1)
                for i in range(n * FC, (n + 1) * FC):
                    V.bn_stats(stf[:, i, :], xn3all[:, i * D:(i + 1) * D]).then_inc(s_rawf, 1)
                for i in range(n * FC, (n + 1) * FC):
                    dve.wait_ge(s_rawf, i + 1)
                    V.bn_aggr(mvf[:, i, :], stf[:, i, :]).then_inc(s_stf, 1)

            def chunk_out(n):
                at = slice(n * FC * D, (n + 1) * FC * D)
                dve.wait_ge(s_norm, (n + 1) * FC)
                dve.wait_ge(s_xb, n + 1)
                r3 = xn3all[:, at].rearrange("p (s d) -> p s d", d=D)
                V.tensor_tensor(r3, r3, gammar[:, :].unsqueeze(1).to_broadcast([P, FC, D]), ALU.mult).then_inc(s_gam, 1)
                dve.wait_ge(s_gam, n + 1)
                V.tensor_tensor(x2all[:, at], xn3all[:, at], x2all[:, at], ALU.add).then_inc(s_fin, 1)

            for n in range(SEQS // FC):
                chunk_sums(n)
                if n:
                    chunk_out(n - 1)
            chunk_out(SEQS // FC - 1)

        @block.gpsimd
        def _(pool):
            G = nc.gpsimd
            pool.dma_start(filler[:, :], fill).then_inc(s_scat, 16)
            G.memset(pay[:, :, :, :], 0.0).then_inc(s_none, 1)
            G.memset(destf[:, :, :], float(SPARE)).then_inc(s_none, 1)
            pool.wait_ge(s_none, 2)
            G.tensor_copy(dest[:, :, :], destf[:, :, :]).then_inc(s_pay, 1)
            G.memset(va[:, :, :, :], 0.0).then_inc(s_set, 1)
            G.memset(va2[:, :, :, :], 0.0).then_inc(s_set, 1)
            G.memset(nmp[:, :, :], 0.0).then_inc(s_set, 1)
            G.memset(onesb[:, :], 1.0).then_inc(s_set, 1)
            G.memset(seenb[:, :], 0.0).then_inc(s_set, 1)
            G.memset(seen[:, :], 0.0).then_inc(s_seen, 1)
            G.memset(half[:, :], -0.5).then_inc(s_set, 1)
            G.memset(minus1[:, :], -1.0).then_inc(s_set, 1)
            G.memset(halff[:, :], -0.5).then_inc(s_set, 1)
            pool.wait_ge(s_set, SET_STEPS - 2)
            G.memset(va[:, :, :, HD], 1.0).then_inc(s_set, 1)
            G.memset(va2[:, :, :, HD], 1.0).then_inc(s_set, 1)
            pool.wait_ge(s_set, SET_STEPS)
            pool.wait_ge(s_cb, 2)

            def norm_group(g):
                wait_alone(pool, s_st1, g * GS + GS)
                G.tensor_scalar(ve1[:, :], mv1[:, :, 1], EPS, None, ALU.add).then_inc(s_nrm1, 1)
                wait_alone(pool, s_nrm1, g * 2 + 1)
                G.tensor_tensor(rs1[:, :], ve1[:, :], half[:, :], ALU.pow).then_inc(s_nrm1, 1)

            def add_bias(g):
                wait_alone(pool, s_xn1, g * GS + GS)
                G.tensor_tensor(xc[:, :, :], xin[:, :, :], cself[:, :].unsqueeze(1).to_broadcast([P, GS, D]),
                                ALU.add).then_inc(s_xfree, 1)

            def parts(g, k):
                wait_alone(pool, s_rhi, g * 2 + k + 1)
                G.tensor_tensor(rlo[:, k, :], rsum[:, k, :], rhi[:, k, :], ALU.subtract).then_inc(s_parts, 1)

            def norm_instance(g, t):
                i = t % GS
                wait_alone(pool, s_x1, done(g, t))
                G.tensor_scalar(ve2[:, :], mv2[:, 1:2], EPS, None, ALU.add).then_inc(s_nrm2, 1)
                wait_alone(pool, s_nrm2, g * (2 * INST) + 2 * t + 1)
                G.tensor_tensor(rs2[:, :], ve2[:, :], half[:, 0:1], ALU.pow).then_inc(s_nrm2, 1)
                wait_alone(pool, s_nrm2, g * (2 * INST) + 2 * t + 2)
                if t < GS:
                    G.tensor_scalar(xn2[:, i, :], x1[:, i, :], mv2[:, 0:1], rs2[:, :],
                                    ALU.subtract, ALU.mult).then_inc(s_xn2, 1)
                    G.tensor_tensor(x1c[:, i, :], x1[:, i, :], ccross[:, :], ALU.add).then_inc(s_x1c, 1)
                else:
                    if i == 0:
                        wait_alone(pool, s_scat, (g + 1) * (16 * GS * TOPK) + 16)
                        wait_alone(pool, s_keep, g * 32 + 16)
                    G.tensor_scalar(pay[:, i, 0, 0:D], x2g[:, i, :], mv2[:, 0:1], rs2[:, :],
                                    ALU.subtract, ALU.mult).then_inc(s_xn2, 1)

            PLACE = 10

            def place_tokens(ph, g):
                n = 0

                def did(ins):
                    nonlocal n
                    n += 1
                    ins.then_inc(s_place, 1)
                    wait_alone(pool, s_place, g * PLACE + n)

                wait_alone(pool, s_gexp, g + 1)
                did(G.tensor_scalar(gden[:, :], gexp[:, :], 1.0, None, ALU.add))
                did(G.tensor_tensor(pay[:, :, 0, D], gden[:, :], minus1[:, :], ALU.pow))
                did(G.tensor_tensor(pay[:, :, 1, D], gexp[:, :], pay[:, :, 0, D], ALU.mult))
                bank, c = ph.item("pos")
                wait_alone(pool, s_wf[bank], c)
                wait_alone(pool, s_rowid, g + 1)
                wait_alone(pool, s_copy, g * GS + GS)
                did(G.tensor_tensor(gsum[:, :, :], hotb[:, 0:2, :], hotb[:, 2:4, :], ALU.add))
                did(G.tensor_tensor(seen[:, :], seen[:, :], gsum[:, 0, :], ALU.add))
                did(G.tensor_tensor(seen[:, :], seen[:, :], gsum[:, 1, :], ALU.add))
                G.tensor_copy(seenb[:, :], seen[:, :]).then_inc(s_seen, 1)
                did(G.tensor_tensor(picked[:, :, :, :], hot[:, :, :, :],
                                    slot[:, :, :].unsqueeze(2).to_broadcast([P, GS, TOPK, E]), ALU.mult))
                did(G.tensor_tensor(picked[:, :, :, 0:4], picked[:, :, :, 0:4], picked[:, :, :, 4:8], ALU.add))
                did(G.tensor_tensor(picked[:, :, :, 0:2], picked[:, :, :, 0:2], picked[:, :, :, 2:4], ALU.add))
                did(G.tensor_tensor(destf[:, :, :], picked[:, :, :, 0], picked[:, :, :, 1], ALU.add))
                G.tensor_copy(dest[:, :, :], destf[:, :, :]).then_inc(s_pay, 1)
                assert n == PLACE

            def scatter(g, some):
                wait_alone(pool, s_pay, g + 1)
                for i in some:
                    for k in range(TOPK):
                        pool.indirect_dma_start(
                            out=routed, out_offset=bass.IndirectOffsetOnAxis(ap=dest[:, i, k:k + 1].bitcast(U32), axis=0),
                            in_=pay[:, i, k, :], in_offset=None, bounds_check=SPARE - 1, oob_is_err=False).then_inc(s_scat, 16)

            def step(ph, g, gp, t):
                if ph.kind == "body":
                    if t == 2:
                        norm_group(g + 1)
                    if t in (4, 5):
                        parts(g + 1, t - 4)
                if not is_first(ph, t):
                    norm_instance(*prv(g, gp, t))
                if t == 1 and gp is not None:
                    place_tokens(ph, gp)
                if ph.kind == "body" and t == 5:
                    add_bias(g + 1)
                if t in (3, 4):
                    scatter(g, range(2 * (t - 3), 2 * (t - 2)))

            norm_group(0)
            add_bias(0)
            for k in range(2):
                parts(0, k)
            after = all_steps(pool, step)
            norm_instance(NG - 1, INST - 1)
            place_tokens(after, NG - 1)
            scatter(NG, range(GS))

            pool.wait_ge(s_keep, 32 * NG + 16)
            wait_alone(pool, s_fill, 16 * (E + 1))
            for n in range(SEQS // FC):
                r = x2all[:, n * FC * D:(n + 1) * FC * D].rearrange("p (s d) -> p s d", d=D)
                G.tensor_tensor(r, r, betar[:, :].unsqueeze(1).to_broadcast([P, FC, D]), ALU.add).then_inc(s_xb, 1)

            def turn(m, c, has):
                if has(-1):
                    n, k, r = m * ROUND + c - 1, (c - 1) % 4, (c - 1) % ROUND
                    wait_alone(pool, s_ys, n + 1)
                    if has(-5):
                        wait_alone(pool, s_sc[k], (m * 2 + (c - 1) // 4) * 16)
                    G.tensor_scalar(yw[:, k, :], ys[:, (c - 1) % 2, :], xr[:, r, D:D + 1], None, ALU.mult).then_inc(s_yw, 1)
                    wait_alone(pool, s_yw, n + 1)
                    pool.indirect_dma_start(
                        out=expert_out, out_offset=bass.IndirectOffsetOnAxis(ap=xr[:, r, D + 1:D + 2].bitcast(U32), axis=0),
                        in_=yw[:, k, :], in_offset=None, bounds_check=YROWS - 1, oob_is_err=False).then_inc(s_sc[k], 16)

            expert_turns(pool, turn)

            for n in range(SEQS // FC):
                at = slice(n * FC, (n + 1) * FC)
                wait_alone(pool, s_stf, (n + 1) * FC)
                G.tensor_scalar(rsf[:, 1, at], mvf[:, at, 1], EPS, None, ALU.add).then_inc(s_rsf, 1)
                wait_alone(pool, s_rsf, 3 * n + 1)
                G.tensor_tensor(rsf[:, 0, at], rsf[:, 1, at], halff[:, at], ALU.pow).then_inc(s_rsf, 1)
                wait_alone(pool, s_rsf, 3 * n + 2)
                G.tensor_tensor(rsf[:, 1, at], mvf[:, at, 0], rsf[:, 0, at], ALU.mult).then_inc(s_rsfm, 1)
                wait_alone(pool, s_rsfm, n + 1)
                G.tensor_scalar(rsf[:, 1, at], rsf[:, 1, at], -1.0, None, ALU.mult).then_inc(s_rsf, 1)

ARRAYS = ("x", "ctx_t", "w_self", "b_self", "bp", "w_cross", "b_cross", "bo", "wg", "bg", "w1", "b1", "w2", "b2",
          "gamma", "beta", "cos_t", "sin_t", "sel_q", "sel_k", "ones_rows", "ident", "ident_bf", "upper", "ebase",
          "row_id", "tile_edge", "fill")


def layout(inputs):
    import numpy as np
    g = {k: np.asarray(v) for k, v in inputs.items()}
    bf16 = mybir.dt.np(BF16)
    swap = np.arange(D) ^ 1
    a = {"x": g["x"], "ctx_t": np.ascontiguousarray(g["ctx_1024"].transpose(2, 0, 1).reshape(D, SEQS * LC))}
    n = "L0_attn_"
    wq, wk = g[n + "Wq"], g[n + "Wk"]
    a["w_self"] = np.stack([wq, wq[:, swap], wk, wk[:, swap], g[n + "Wv"], g[n + "Wp"]], 1)
    a["b_self"] = np.stack([g[n + "bq"], g[n + "bq"][swap], g[n + "bk"], g[n + "bk"][swap], g[n + "bv"]], 1)
    a["bp"] = g[n + "bp"]
    n = "L0_xattn_"
    a["w_cross"] = np.stack([g[n + w].T for w in ("Wq", "Wk", "Wv", "Wo")], 1)
    a["b_cross"] = np.stack([g[n + b] for b in ("bq", "bk", "bv")], 1)
    a["bo"] = g[n + "bo"]
    n = "L0_ffn_"
    a["wg"], a["bg"] = g[n + "Wg"], g[n + "bg"]
    a["w1"], a["w2"], a["b2"] = g[n + "W1"], g[n + "W2"], g[n + "b2"]
    a["b1"] = g[n + "b1"].reshape(E, HC, P).transpose(2, 0, 1).reshape(P, E * HC)
    a["gamma"], a["beta"] = g[n + "gamma"], g[n + "beta"]
    inv = (np.float32(1.0) / np.float32(10000.0) ** (np.arange(0, HD, 2, dtype=np.float32) / np.float32(HD))).astype(np.float32)
    freq = np.arange(L, dtype=np.float32)[:, None] * inv
    pairs = (np.arange(D) % HD) // 2
    sign = np.where(np.arange(D) % 2, 1.0, -1.0).astype(np.float32)
    a["cos_t"] = np.cos(freq)[:, pairs].T.astype(np.float32)
    a["sin_t"] = (np.sin(freq)[:, pairs].T * sign[:, None]).astype(np.float32)
    sel = np.zeros((2, P, 2, NB, P), np.float16)
    for j in range(NJ):
        for b in range(NB):
            for c in range(4):
                for d in range(HD):
                    r, at = 32 * j + HD * c + d, (NB * j + b) * HD + d
                    sel[0, at, c // 2, b, r] = 1
                    sel[1, at, c % 2, b, r] = 1
    a["sel_q"], a["sel_k"] = sel[0], sel[1]
    rows = np.zeros((P, NJ, NB, P), bf16)
    for j in range(NJ):
        for b in range(NB):
            rows[32 * j + b, j, b, :] = rows[32 * j + NB + b, j, b, :] = 1
    a["ones_rows"] = rows
    a["ident"] = np.eye(P, dtype=np.float32)
    a["ident_bf"] = np.eye(P).astype(bf16)
    a["upper"] = np.triu(np.ones((P, P)), 1).astype(bf16)
    a["ebase"] = np.broadcast_to(np.stack([np.arange(E) * REGION, np.arange(E)]).astype(np.float32), (P, 2, E))
    token = np.arange(SEQS)[None, :, None] * L + np.arange(P)[:, None, None]
    a["row_id"] = (token + np.arange(TOPK)[None, None, :] * NTOK).astype(np.int32)
    a["tile_edge"] = np.concatenate([np.arange(SEQS) * P, np.arange(NT)]).astype(np.float32)[None]
    fill = np.zeros((P, PAYW), np.float32)
    fill[:, D + 1] = np.full(P, YROWS, np.int32).view(np.float32)
    a["fill"] = fill
    return {k: np.ascontiguousarray(a[k]) for k in ARRAYS}


def kernel(**inputs):
    import concourse.bacc as _bacc
    from concourse import mybir as _mybir
    from concourse.bass_utils import run_bass_kernel_spmd as _run

    arrays = layout(inputs)
    nc = _bacc.Bacc("TRN2", target_bir_lowering=False, num_devices=1)
    args = [nc.dram_tensor(n, a.shape, _mybir.dt.from_np(a.dtype), kind="ExternalInput").ap() for n, a in arrays.items()]
    args.append(nc.dram_tensor("out", (SEQS, L, D), F32, kind="ExternalOutput").ap())
    decoder_layer(nc, *args)
    return _run(nc, [arrays], core_ids=[0]).results[0]["out"]
```

```python
import concourse.bass as bass
from concourse import mybir
from contextlib import ExitStack

F32 = mybir.dt.float32
F16 = mybir.dt.float16
BF16 = mybir.dt.bfloat16
I32 = mybir.dt.int32
U32 = mybir.dt.uint32
ALU = mybir.AluOpType
ACT = mybir.ActivationFunctionType
AX = mybir.AxisListType

P = 128
SEQS, L, D, LC = 32, 128, 128, 77
H, HD = 16, 8
GS = 4
NG = SEQS // GS
TOK = GS * L
CTOK = GS * LC
NJ, NB = 4, 4
VW = 32
INST = 2 * GS
SCALE = 1.0 / 8.0 ** 0.5
EPS = 1e-5
E, HID = 8, 512
NTOK = SEQS * L
TOPK = 2
HC = HID // P
REGION = NTOK + P
ROUND = 8
NT = -(-((NTOK * TOPK) // P + E - 1) // ROUND) * ROUND
PAYW = D + 2
SPARE = E * REGION
YROWS = TOPK * NTOK

BACKGROUND = {
    (2, 0): [("v2", 0, "own")], (2, 1): [("x2t0", 1, "q2")], (2, 2): [("q20", 0, "q2")], (2, 3): [("gq20", 1, "q2")],
    (3, 0): [("xnt", 0, "next")], (3, 1): [("x2t1", 1, "q2"), ("q", 0, "next")],
    (3, 2): [("q21", 0, "q2"), ("rq", 1, "next")], (3, 3): [("gq21", 1, "q2"), ("k", 0, "next")],
    (4, 0): [("rk", 1, "next")], (4, 1): [("x2t2", 1, "q2")], (4, 2): [("q22", 0, "q2")],
    (4, 3): [("v", 0, "next"), ("gq22", 1, "q2")],
    (5, 0): [("gq0", 0, "next")], (5, 1): [("gq1", 0, "next"), ("x2t3", 1, "q2")],
    (5, 2): [("gq2", 1, "next"), ("q23", 0, "q2")], (5, 3): [("gq3", 0, "next"), ("gq23", 1, "q2")],
    (6, 0): [("gk0", 0, "next")], (6, 1): [("gk1", 1, "next")], (6, 2): [("gk2", 0, "next"), ("x3t0", 1, "x3")],
    (6, 3): [("gk3", 0, "next")],
    (7, 2): [("x3t1", 1, "x3")],
    (0, 0): [("k2", 0, "own")], (0, 2): [("gk20", 0, "own"), ("x3t2", 1, "tail")], 
    (1, 0): [("x3t3", 1, "tail"), ("gk21", 0, "own")], (1, 1): [("log", 0, "tail"), ("gk22", 1, "own")],
    (1, 2): [("gk23", 0, "own")], (1, 3): [("pos", 1, "tail")],
}


def items_at(t, j, kinds):
    return [(n, b) for n, b, kind in BACKGROUND.get((t, j), []) if kind in kinds]


def order_of(steps, kinds_of):
    return [it for t in steps for j in range(NJ) for it in items_at(t, j, kinds_of(t))]


NEXT_ITEMS = [it for t in range(2, 8) for j in range(NJ) for it in items_at(t, j, ("next",))]
TAIL_ITEMS = order_of((0, 1), lambda t: ("tail",))
PRO_ORDER = NEXT_ITEMS + order_of((0, 1), lambda t: ("own",))
BODY_ORDER = order_of((2, 3, 4, 5, 6, 7), lambda t: ("q2", "next", "x3", "own")) + order_of((0, 1), lambda t: ("own", "tail"))
LAST_ORDER = order_of((2, 3, 4, 5, 6, 7), lambda t: ("q2", "x3", "own")) + order_of((0, 1), lambda t: ("tail",))


class Phase:

    def __init__(self, kind, g):
        self.kind, self.g = kind, g
        self.order = {"before": PRO_ORDER, "body": BODY_ORDER, "after": LAST_ORDER}[kind]

    def item(self, name):
        bank = dict(self.order)[name]
        on_bank = [n for n, b in self.order if b == bank]
        before = sum(b == bank for _, b in PRO_ORDER)
        body = sum(b == bank for _, b in BODY_ORDER)
        base = 0 if self.kind == "before" else self.g * body + before
        return bank, base + on_bank.index(name) + 1

    def kinds(self, t):
        if self.kind == "before":
            return ("own",)
        if t < 2:
            return ("own", "tail")
        return ("q2", "next", "x3", "own") if self.kind == "body" else ("q2", "x3", "own")

    def at(self, t, j):
        return [(n, kind) for n, _, kind in BACKGROUND.get((t, j), []) if kind in self.kinds(t)]


def decoder_layer(nc, x, ctx_t, w_self, b_self, bp, w_cross, b_cross, bo, wg, bg, w1, b1, w2, b2,
                  gamma, beta, cos_t, sin_t, sel_q, sel_k, ones_rows, ident, ident_bf, upper, ebase,
                  row_id, tile_edge, fill, out):
    stack = ExitStack()
    with stack:
        def sb(name, shape, dt=F32):
            return stack.enter_context(nc.sbuf_tensor(name, shape, dt))

        def pb(name, shape, dt=F32):
            return stack.enter_context(nc.psum_tensor(name, shape, dt))

        def sem(name):
            return stack.enter_context(nc.semaphore(name))

        x_rows = x.rearrange("(g i) l d -> l g i d", i=GS)
        out_rows = out.rearrange("s l d -> l s d")

        routed = nc.dram_tensor("routed", (SPARE + P, PAYW), F32, kind="Internal").ap()
        expert_out = nc.dram_tensor("expert_out", (YROWS + P, D), F32, kind="Internal").ap()

        wself = sb("wself", [P, 6, D])
        wcross = sb("wcross", [P, 4, D])
        bself = sb("bself", [P, 5])
        bcross = sb("bcross", [P, 3])
        cosb = sb("cosb", [P, L])
        sinb = sb("sinb", [P, L])
        selq = sb("selq", [P, 2, NB, P], F16)
        selk = sb("selk", [P, 2, NB, P], F16)
        onesr = sb("onesr", [P, NJ, NB, P], BF16)
        idf = sb("idf", [P, P])
        idb = sb("idb", [P, P], BF16)
        upperb = sb("upperb", [P, P], BF16)
        onesb = sb("onesb", [P, P], BF16)
        bprow = sb("bprow", [P, D])
        borow = sb("borow", [P, D])
        cself = sb("cself", [P, D])
        ccross = sb("ccross", [P, D])
        bvb = sb("bvb", [P, 2, P])
        wgs = sb("wgs", [P, E])
        bgrow = sb("bgrow", [P, E])
        etab = sb("etab", [P, 2, E])
        ebaser, iota8 = etab[:, 0, :], etab[:, 1, :]
        rowid = sb("rowid", [P, SEQS, TOPK], I32)
        half = sb("half", [P, GS])

        xin = sb("xin", [P, GS, D])
        ctxb = sb("ctxb", [P, CTOK])
        st1 = sb("st1", [P, GS, 6])
        mv1 = sb("mv1", [P, GS, 2])
        rs1 = sb("rs1", [P, GS])
        ve1 = sb("ve1", [P, GS])
        xn1 = sb("xn1", [P, GS, D])
        xc = sb("xc", [P, GS, D])
        xnt = sb("xnt", [P, TOK])
        ra = sb("ra", [P, 2, TOK])
        rb = sb("rb", [P, 2, TOK])
        rsum = sb("rsum", [P, 2, TOK])
        rhi = sb("rhi", [P, 2, TOK], F16)
        rlo = sb("rlo", [P, 2, TOK], F16)
        qs = sb("qs", [P, NB, TOK], F16)
        ks = sb("ks", [P, NB, TOK], F16)
        va = sb("va", [P, GS, H, VW])
        k2hi = sb("k2hi", [P, CTOK], F16)
        k2lo = sb("k2lo", [P, CTOK], F16)
        k2s = sb("k2s", [P, NB, CTOK], F16)
        va2 = sb("va2", [P, GS, H, VW])
        x1 = sb("x1", [P, GS, D])
        x1c = sb("x1c", [P, GS, D])
        st2 = sb("st2", [P, 6])
        mv2 = sb("mv2", [P, 2])
        ve2 = sb("ve2", [P, 1])
        rs2 = sb("rs2", [P, 1])
        xn2 = sb("xn2", [P, GS, D])
        x2t = sb("x2t", [P, L])
        q2hi = sb("q2hi", [P, L], F16)
        q2lo = sb("q2lo", [P, L], F16)
        q2s = sb("q2s", [P, GS, NB, L], F16)
        nm = sb("nm", [P, NJ, NB])
        nmp = sb("nmp", [P, NJ, 32], BF16)
        nmt = sb("nmt", [P, P], BF16)
        prob = sb("prob", [P, NJ, NB * L])
        ots = sb("ots", [P, NJ * L])
        rden = sb("rden", [P, H])
        onorm = sb("onorm", [P, H, HD])
        onormt = sb("onormt", [P, L])
        x2g = sb("x2g", [P, GS, D])
        x2all = sb("x2all", [P, SEQS * D])
        xn3all = sb("xn3all", [P, SEQS * D])
        xn3t = sb("xn3t", [P, TOK])
        pay = sb("pay", [P, GS, TOPK, PAYW])
        lg = sb("lg", [P, GS, E])
        top = sb("top", [P, GS, 8])
        topi = sb("topi", [P, GS, 8], U32)
        topf = sb("topf", [P, GS, TOPK])
        hot = sb("hot", [P, GS, TOPK, E])
        hotb = sb("hotb", [P, GS, E], BF16)
        gap = sb("gap", [P, GS])
        gexp = sb("gexp", [P, GS])
        gden = sb("gden", [P, GS])
        minus1 = sb("minus1", [P, GS])
        seen = sb("seen", [P, E])
        seenb = sb("seenb", [P, E], BF16)
        gsum = sb("gsum", [P, 2, E])
        slot = sb("slot", [P, GS, E])
        picked = sb("picked", [P, GS, TOPK, E])
        destf = sb("destf", [P, GS, TOPK])
        dest = sb("dest", [P, GS, TOPK], I32)

        w1s = sb("w1s", [P, E * HID])
        w2s = sb("w2s", [P, E * HID])
        b1s = sb("b1s", [P, E * HC])
        b2row = sb("b2row", [P, E * D])
        edges = sb("edges", [1, SEQS + NT])
        filler = sb("filler", [P, PAYW])
        counts = sb("counts", [1, E])
        countsi = sb("countsi", [1, E], I32)
        over = sb("over", [1, E, SEQS])
        tiles = sb("tiles", [1, 3, E])
        ones8 = sb("ones8", [1, E])
        isof = sb("isof", [1, 2, NT, E])
        tabf = sb("tabf", [1, 4, NT])
        tab = sb("tab", [1, 4, NT], I32)
        xr = prob[:, :, :].rearrange("p j c -> p (j c)")[:, 0:ROUND * PAYW].rearrange("p (r c) -> p r c", c=PAYW)
        xt = sb("xt", [P, 2, P])
        w1c = sb("w1c", [P, 2, HID])
        ht = sb("ht", [P, 2, HC, P])
        ys = sb("ys", [P, 2, D])
        yw = sb("yw", [P, 4, D])
        FC = 4
        CHUNKS = SEQS // FC
        y2 = [v[:, :, :, :].rearrange("p i h c -> p (i h c)").rearrange("p (r k n) -> p r k n", r=2, k=TOPK)[:, r]
              for v in (va, va2) for r in range(2)]
        stf = sb("stf", [P, SEQS, 6])
        mvf = sb("mvf", [P, SEQS, 2])
        rsf = sb("rsf", [P, 2, SEQS])
        nmf = sb("nmf", [P, SEQS])
        halff = sb("halff", [P, SEQS])
        gammar = sb("gammar", [P, D])
        betar = sb("betar", [P, D])

        S = [pb(f"S{i}", [P, 512]) for i in range(2)]
        ST = [pb(f"ST{i}", [P, 512]) for i in range(2)]
        AV = pb("AV", [P, 512])
        SM = pb("SM", [P, 512])
        W = [pb(f"W{i}", [P, 512]) for i in range(2)]
        SUM = (S[0], S[1], ST[0], ST[1])
        SMb = SM[:, 0:64].bitcast(BF16)

        s_ready = sem("s_ready")
        s_first = sem("s_first")
        s_const = sem("s_const")
        s_x = sem("s_x")
        s_ctx = sem("s_ctx")
        s_set = sem("s_set")
        s_cb = sem("s_cb")
        s_xfree = sem("s_xfree")
        s_S = sem("s_S")
        s_max = sem("s_max")
        s_nmp = sem("s_nmp")
        s_sm = sem("s_sm")
        s_smf = sem("s_smf")
        s_st = sem("s_st")
        s_exp = sem("s_exp")
        s_av = sem("s_av")
        s_ot = sem("s_ot")
        s_w = [sem(f"s_w{i}") for i in range(2)]
        s_wf = [sem(f"s_wf{i}") for i in range(2)]
        s_bvb = sem("s_bvb")
        s_cbp = sem("s_cbp")
        s_raw1 = sem("s_raw1")
        s_st1 = sem("s_st1")
        s_nrm1 = sem("s_nrm1")
        s_raw2 = sem("s_raw2")
        s_nrm2 = sem("s_nrm2")
        s_neg = sem("s_neg")
        s_rden = sem("s_rden")
        s_sum = sem("s_sum")
        s_rhi = sem("s_rhi")
        s_route = sem("s_route")
        s_k2hi = sem("s_k2hi")
        s_q2hi = sem("s_q2hi")
        s_xn1 = sem("s_xn1")
        s_parts = sem("s_parts")
        s_x1 = sem("s_x1")
        s_xn2 = sem("s_xn2")
        s_gap = sem("s_gap")
        s_gexp = sem("s_gexp")
        s_keep = sem("s_keep")
        s_pay = sem("s_pay")
        s_rowid = sem("s_rowid")
        s_place = sem("s_place")
        s_last = sem("s_last")
        s_seen = sem("s_seen")
        s_copy = sem("s_copy")
        s_x1c = sem("s_x1c")
        s_none = sem("s_none")
        s_hot = sem("s_hot")
        s_scat = sem("s_scat")

        def done(g, t, per=1, c=0):
            return g * (INST * per) + t * per + c + 1

        def sm_count(g, t, what, ended=False):
            c = {"maxima": -2, "sums": 3, "normed": 4, "projected": 5}[what] - (1 if ended else 0)
            if what == "maxima" and is_zero(g, t):
                c = 1
            return g * (INST * 4) + t * 4 + c

        def is_zero(g, t):
            return isinstance(g, int) and g == 0 and t == 0

        def nxt(g, t):
            return (g, t + 1) if t + 1 < INST else (g + 1, 0)

        def prv(g, gp, t):
            return (g, t - 1) if t else (gp, INST - 1)

        def is_first(ph, t):
            return ph.kind == "before" and t == 0

        def is_last(ph, t):
            return ph.kind == "after" and t == INST - 1

        def wait_alone(eng, s, value):
            if not isinstance(value, int):
                eng.compute_val(value)
            eng.wait_ge(s_ready, 1)
            eng.wait_ge(s, value)

        def group_of(kind, g, gp):
            return {"next": g + 1, "tail": gp}.get(kind, g)

        def expert_turns(eng, turn):
            for i in range(-2, ROUND + 1):
                turn(0, i, lambda k, i=i: i + k >= 0)
            with eng.Fori(1, NT // ROUND - 1) as m:
                for c in range(1, ROUND + 1):
                    turn(m, c, lambda k: True)
            for c in range(1, ROUND + 1):
                turn(NT // ROUND - 1, c, lambda k, c=c: NT - ROUND + c + k < NT)

        def times_gamma(eng, n):
            r3 = xn3all[:, n * FC * D:(n + 1) * FC * D].rearrange("p (s d) -> p s d", d=D)
            eng.tensor_tensor(r3, r3, gammar[:, :].unsqueeze(1).to_broadcast([P, FC, D]), ALU.mult).then_inc(s_gam[n % 2], 1)

        def keys(t):
            return L if t < GS else LC

        def all_steps(eng, step):
            before = Phase("before", 0)
            for t in range(2):
                step(before, 0, None, t)
            with eng.Fori(0, NG - 1) as g:
                body = Phase("body", g)
                for t in range(2, INST):
                    step(body, g, None, t)
                for t in range(2):
                    step(body, g + 1, g, t)
            after = Phase("after", NG - 1)
            for t in range(2, INST):
                step(after, NG - 1, None, t)
            return after

        s_wts = sem("s_wts")
        s_cnt = sem("s_cnt")
        s_cnti = sem("s_cnti")
        s_fill = sem("s_fill")
        s_tabs = sem("s_tabs")
        s_tab = sem("s_tab")
        s_xr = [sem(f"s_xr{i}") for i in range(ROUND)]
        s_xp = sem("s_xp")
        s_xt = sem("s_xt")
        s_h = sem("s_h")
        s_gelu = sem("s_gelu")
        s_y = sem("s_y")
        s_ys = sem("s_ys")
        s_yw = sem("s_yw")
        s_sc = [sem(f"s_sc{i}") for i in range(4)]
        s_xb = sem("s_xb")
        s_y2 = [[sem(f"s_y2{k}{i}") for i in range(4)] for k in range(TOPK)]
        s_add = sem("s_add")
        s_nmean = sem("s_nmean")
        s_rawf = sem("s_rawf")
        s_stf = sem("s_stf")
        s_rsf = sem("s_rsf")
        s_norm = sem("s_norm")
        s_rsfm = sem("s_rsfm")
        s_gam = [sem(f"s_gam{i}") for i in range(2)]
        s_fin = sem("s_fin")
        s_out = sem("s_out")

        FIRST = (
            (idf[:, :], ident), (wself[:, :, :], w_self), (bself[:, :], b_self), (cosb[:, :], cos_t),
            (sinb[:, :], sin_t),
        )
        CONSTS = (
            (selq[:, :, :, :], sel_q), (selk[:, :, :, :], sel_k),
            (idb[:, :], ident_bf), (onesr[:, :, :, :], ones_rows), (wcross[:, :, :], w_cross),
            (bcross[:, :], b_cross), (upperb[:, :], upper), (etab[:, :, :], ebase), (wgs[:, :], wg),
            (rowid[:, :, :], row_id), (bprow[:, :], bp.partition_broadcast(P)),
            (borow[:, :], bo.partition_broadcast(P)), (bgrow[:, :], bg.partition_broadcast(P)),
            (b1s[:, :], b1),
            (b2row[:, :], b2.rearrange("e d -> (e d)").partition_broadcast(P)),
            (gammar[:, :], gamma.partition_broadcast(P)), (betar[:, :], beta.partition_broadcast(P)),
        )
        SET_STEPS = 9

        block = stack.enter_context(nc.Block())


        @block.sync
        def _(sp):
            sp.dma_start(xin[:, :, :], x_rows[:, 0, :, :]).then_inc(s_x, 16)
            for dst, src in FIRST:
                sp.dma_start(dst, src).then_inc(s_first, 16)
            for dst, src in CONSTS:
                sp.dma_start(dst, src).then_inc(s_const, 16)
            sp.dma_start(ctxb[:, :], ctx_t[:, 0:CTOK]).then_inc(s_ctx, 16)
            sp.dma_start(edges[:, :], tile_edge).then_inc(s_keep, 16)
            for e in range(E):
                at = slice(e * HID, (e + 1) * HID)
                sp.dma_start(w1s[:, at], w1[e, :, :]).then_inc(s_wts, 16)
                sp.dma_start(w2s[:, at].rearrange("p (c d) -> p c d", d=D),
                             w2[e, :, :].rearrange("(c p) d -> p c d", p=P)).then_inc(s_wts, 16)

            def keep(g):
                sp.wait_ge(s_xn2, done(g, INST - 1))
                at = bass.ds(g * (GS * D), GS * D)
                sp.dma_start(x2all[:, at], x2g[:, :, :].rearrange("p i d -> p (i d)")).then_inc(s_keep, 16)
                sp.dma_start(xn3all[:, at].rearrange("p (i d) -> p i d", d=D), pay[:, :, 0, 0:D]).then_inc(s_keep, 16)

            with sp.Fori(0, NG - 1) as g:
                sp.wait_ge(s_xfree, g + 1)
                sp.dma_start(xin[:, :, :], x_rows[:, bass.ds(g + 1, 1), :, :].rearrange("l a i d -> l (a i) d")).then_inc(s_x, 16)
                sp.wait_ge(s_q2hi, g * GS + 1)
                sp.dma_start(ctxb[:, :], ctx_t[:, bass.ds((g + 1) * CTOK, CTOK)]).then_inc(s_ctx, 16)
                keep(g)
            keep(NG - 1)
            sp.wait_ge(s_scat, 16)
            sp.dma_start(routed[SPARE:SPARE + P, :], filler[:, :]).then_inc(s_fill, 16)
            sp.wait_ge(s_cnti, 1)
            for e in range(E):
                c = sp.value_load(countsi[0:1, e:e + 1], min_val=0, max_val=NTOK)
                sp.dma_start(routed[bass.ds(c + e * REGION, P), :], filler[:, :]).then_inc(s_fill, 16)
            sp.wait_ge(s_fill, 16 * (E + 1))
            sp.wait_ge(s_scat, 16 * (NG + 1) * GS * TOPK + 16)
            sp.wait_ge(s_tab, 1)

            def load(m, c):
                row = sp.value_load(tab[0:1, 1, bass.ds(m * ROUND + c, 1)], min_val=0, max_val=SPARE)
                sp.dma_start(xr[:, c, :], routed[bass.ds(row, P), :]).then_inc(s_xr[c], 16)

            for c in range(ROUND):
                load(0, c)
            with sp.Fori(1, NT // ROUND) as m:
                for c in range(ROUND):
                    sp.wait_ge(s_sc[c % 4], m * 32 - 16 + 16 * (c // 4))
                    load(m, c)
            for k in range(4):
                sp.wait_ge(s_sc[k], 16 * NT // 4)
            for n in range(CHUNKS):
                if n >= 4:
                    sp.wait_ge(s_add, n - 3)
                for k in range(TOPK):
                    r0 = k * NTOK + n * FC * L
                    sp.dma_start(y2[n % 4][:, k, :].rearrange("p (s d) -> p s d", d=D),
                                 expert_out[r0:r0 + FC * L, :].rearrange("(s p) d -> p s d", p=P)).then_inc(s_y2[k][n % 4], 16)
            for n in range(CHUNKS):
                sp.wait_ge(s_fin, n + 1)
                sp.dma_start(out_rows[:, n * FC:(n + 1) * FC, :],
                             x2all[:, n * FC * D:(n + 1) * FC * D].rearrange("p (s d) -> p s d", d=D)).then_inc(s_out, 16)
            sp.wait_ge(s_out, 16 * CHUNKS)

        @block.tensor
        def _(pe):
            mm = nc.tensor.matmul
            tr = nc.tensor.transpose
            pe.wait_ge(s_ready, 1)
            pe.wait_ge(s_first, 16 * len(FIRST))

            def scores(ph, g, t, j):
                first = is_zero(g, t)
                u = done(g, t, NJ, j)
                if j == 0 and t == 0:
                    for name in ("gk3", "gk1"):
                        bank, c = ph.item(name)
                        pe.wait_ge(s_wf[bank], c)
                if j == 0 and t >= GS:
                    bank, c = ph.item(f"gq2{t - GS}")
                    pe.wait_ge(s_wf[bank], c)
                if not (first and j < 2):
                    pe.wait_ge(s_max, u - 2)
                bank = S[j % 2]
                n = keys(t)
                rows = slice(32 * j, 32 * j + 32)
                for b in range(NB):
                    if t < GS:
                        q, k = qs[rows, b, t * L:(t + 1) * L], ks[rows, b, t * L:(t + 1) * L]
                    else:
                        i = t - GS
                        q, k = q2s[rows, i, b, :], k2s[rows, b, i * LC:(i + 1) * LC]
                    last = mm(bank[:, b * n:(b + 1) * n], q, k, start=True, stop=True)
                last.then_inc(s_S, 1)

            def shifted(ph, g, t, j):
                first = is_zero(g, t)
                if j == 0:
                    pe.wait_ge(s_smf, sm_count(g, t, "maxima"))
                if not (first and j < 2):
                    pe.wait_ge(s_exp, done(g, t, NJ, j) - 2)
                n = keys(t)
                rows = slice(32 * j, 32 * j + 32)
                for b in range(NB):
                    o = ST[j % 2][0:n, b * L:(b + 1) * L]
                    if t < GS:
                        q, k = qs[rows, b, t * L:(t + 1) * L], ks[rows, b, t * L:(t + 1) * L]
                    else:
                        i = t - GS
                        q, k = q2s[rows, i, b, :], k2s[rows, b, i * LC:(i + 1) * LC]
                    mm(o, onesr[:, j, b, 0:n], nmt[:, :], start=True, stop=False)
                    last = mm(o, k, q, start=False, stop=True)
                last.then_inc(s_st, 1)

            def values(ph, g, t, j):
                if j == 0 and not is_first(ph, t):
                    pe.wait_ge(s_ot, done(g, t) - 1)
                pe.wait_ge(s_exp, done(g, t, NJ, j))
                n = keys(t)
                v = va if t < GS else va2
                for b in range(NB):
                    last = mm(AV[32 * b:32 * b + 32, j * L:(j + 1) * L], v[0:n, t % GS, NB * j + b, :],
                              prob[0:n, j, b * L:(b + 1) * L], start=True, stop=True)
                last.then_inc(s_av, 1)

            def small(what, g, t, ended=False):
                c = sm_count(g, t, what, ended)
                if not (is_zero(g, t) and what == "maxima"):
                    pe.wait_ge(s_smf, c - 1)
                if what == "maxima":
                    pe.wait_ge(s_nmp, done(g, t))
                    tr(SMb, nmp[:, :, :].rearrange("p j c -> p (j c)"), idb[:, :]).then_inc(s_sm, 1)
                elif what == "sums":
                    pe.wait_ge(s_ot, done(g, t))
                    for j in range(NJ):
                        last = tr(SM[:, j * L:(j + 1) * L], ots[:, j * L:(j + 1) * L], idf[:, :])
                    last.then_inc(s_sm, 1)
                elif what == "normed":
                    tr(SM[:, 0:L], onorm[:, :, :].rearrange("p h c -> p (h c)"), idf[:, :]).then_inc(s_sm, 1)
                else:
                    w = wself[:, 5, :] if t < GS else wcross[:, 3, :]
                    mm(SM[:, 0:D], onormt[:, :], w, start=True, stop=True).then_inc(s_sm, 1)

            def work(ph, g, name):
                bank, c = ph.item(name)
                w = W[bank]
                if not (ph.kind == "before" and c == 1):
                    pe.wait_ge(s_wf[bank], c - 1)
                if name == "xnt":
                    pe.wait_ge(s_xn1, g * GS + GS)
                    for i in range(GS):
                        last = tr(w[:, i * L:(i + 1) * L], xn1[:, i, :], idf[:, :])
                elif name in ("q", "rq", "k", "rk"):
                    fb, fc = ph.item("xnt")
                    pe.wait_ge(s_wf[fb], fc)
                    last = mm(w[:, :], wself[:, ("q", "rq", "k", "rk").index(name), :], xnt[:, :], start=True, stop=True)
                elif name == "v":
                    for i in range(GS):
                        last = mm(w[:, i * D:(i + 1) * D], xnt[:, i * L:(i + 1) * L], wself[:, 4, :], start=True, stop=True)
                elif name[:2] in ("gq", "gk") and name[2] != "2" or name in ("gq2", "gk2"):
                    b, k = int(name[2]), 0 if name[1] == "q" else 1
                    sel = selq if k == 0 else selk
                    pe.wait_ge(s_parts, g * 2 + k + 1)
                    mm(w[:, :], sel[:, 0, b, :], rhi[:, k, :], start=True, stop=False)
                    last = mm(w[:, :], sel[:, 1, b, :], rlo[:, k, :], start=False, stop=True)
                elif name == "k2":
                    pe.wait_ge(s_ctx, g * 16 + 16)
                    last = mm(w[:, 0:CTOK], wcross[:, 1, :], ctxb[:, :], start=True, stop=True)
                elif name == "v2":
                    for i in range(GS):
                        last = mm(w[0:LC, i * D:(i + 1) * D], ctxb[:, i * LC:(i + 1) * LC], wcross[:, 2, :],
                                  start=True, stop=True)
                elif name.startswith("gk2"):
                    b = int(name[3])
                    fb, fc = ph.item("k2")
                    pe.wait_ge(s_wf[fb], fc)
                    mm(w[:, 0:CTOK], selk[:, 0, b, :], k2hi[:, :], start=True, stop=False)
                    last = mm(w[:, 0:CTOK], selk[:, 1, b, :], k2lo[:, :], start=False, stop=True)
                elif name.startswith("x2t"):
                    i = int(name[3])
                    pe.wait_ge(s_xn2, done(g, i))
                    last = tr(w[:, 0:L], xn2[:, i, :], idf[:, :])
                elif name.startswith("q2"):
                    fb, fc = ph.item("x2t" + name[2])
                    pe.wait_ge(s_wf[fb], fc)
                    last = mm(w[:, 0:L], wcross[:, 0, :], x2t[:, :], start=True, stop=True)
                elif name.startswith("gq2"):
                    fb, fc = ph.item("q2" + name[3])
                    pe.wait_ge(s_wf[fb], fc)
                    for b in range(NB):
                        o = w[:, b * L:(b + 1) * L]
                        mm(o, selq[:, 0, b, :], q2hi[:, :], start=True, stop=False)
                        last = mm(o, selq[:, 1, b, :], q2lo[:, :], start=False, stop=True)
                elif name.startswith("x3t"):
                    i = int(name[3])
                    pe.wait_ge(s_xn2, done(g, GS + i))
                    last = tr(w[:, 0:L], pay[:, i, 0, 0:D], idf[:, :])
                elif name == "log":
                    fb, fc = ph.item("x3t3")
                    pe.wait_ge(s_wf[fb], fc)
                    for i in range(GS):
                        last = mm(w[:, i * E:(i + 1) * E], xn3t[:, i * L:(i + 1) * L], wgs[:, :], start=True, stop=True)
                else:
                    pe.wait_ge(s_hot, g + 1)
                    wait_alone(pe, s_seen, g + 1)
                    hb = hotb[:, :, :]
                    mm(w[:, 0:GS * E], upperb[:, :], hb.rearrange("p i e -> p (i e)"), start=True, stop=False)
                    for i in range(1, GS):
                        mm(w[:, i * E:GS * E], onesb[:, :], hb[:, 0:GS - i, :].rearrange("p i e -> p (i e)"),
                           start=False, stop=False)
                    for i in range(GS):
                        last = mm(w[:, i * E:(i + 1) * E], onesb[:, :], seenb[:, :], start=False, stop=(i == GS - 1))
                last.then_inc(s_w[bank], 1)

            def step(ph, g, gp, t):
                for j in range(NJ):
                    if not is_last(ph, t) and 0 < j < 3:
                        scores(ph, *nxt(g, t), j)
                    shifted(ph, g, t, j)
                    if not is_last(ph, t) and j == 0:
                        scores(ph, *nxt(g, t), j)
                    if j:
                        values(ph, g, t, j - 1)
                    if not is_first(ph, t) and j < 3:
                        small(("sums", "normed", "projected")[j], *prv(g, gp, t))
                    if not is_last(ph, t) and j == 2:
                        scores(ph, *nxt(g, t), 3)
                    for name, kind in ph.at(t, j):
                        work(ph, group_of(kind, g, gp), name)
                if not is_last(ph, t):
                    small("maxima", *nxt(g, t))
                values(ph, g, t, NJ - 1)

            before = Phase("before", 0)
            for name, _ in NEXT_ITEMS:
                if name == "gq0":
                    pe.wait_ge(s_const, 16 * len(CONSTS))
                    pe.wait_ge(s_bvb, 2)
                    mm(S[0][:, 0:D], bvb[:, 0, :], wself[:, 5, :], start=True, stop=True).then_inc(s_cbp, 1)
                    mm(S[1][:, 0:D], bvb[:, 1, :], wcross[:, 3, :], start=True, stop=True).then_inc(s_cbp, 1)
                work(before, 0, name)
            pe.wait_ge(s_set, SET_STEPS)
            pe.wait_ge(s_cb, 2)
            for j in range(NJ):
                scores(before, 0, 0, j)
            small("maxima", 0, 0)
            after = all_steps(pe, step)
            for k in ("sums", "normed", "projected"):
                small(k, NG - 1, INST - 1, ended=True)
            for name, _ in TAIL_ITEMS:
                work(after, NG - 1, name)


            pe.wait_ge(s_max, NG * INST * NJ)
            mm(S[0][:, 0:E], onesb[:, :], seenb[:, :], start=True, stop=False)
            for i in range(GS):
                last = mm(S[0][:, 0:E], onesb[:, :], hotb[:, i, :], start=False, stop=(i == GS - 1))
            last.then_inc(s_cnt, 1)
            pe.wait_ge(s_tab, 1)
            pe.wait_ge(s_wts, 16 * 2 * E)

            experts = {}

            def expert_of(m, c):
                if c not in experts:
                    experts[c] = pe.value_load(tab[0:1, 0, bass.ds(m * ROUND + c, 1)], min_val=0, max_val=(E - 1) * HID)
                return experts[c]

            def turn(m, c, has):
                if c == 1:
                    experts.clear()
                e = expert_of(m, c) if has(0) else None
                if has(2):
                    n, k, r = m * ROUND + c + 2, (c + 2) % 2, (c + 2) % ROUND
                    pe.wait_ge(s_xr[r], (m + (c + 2) // ROUND) * 16 + 16)
                    tr(W[k][:, 0:P], xr[:, r, 0:D], idf[:, :]).then_inc(s_xp, 1)
                if has(1):
                    n, k = m * ROUND + c + 1, (c + 1) % 2
                    pe.wait_ge(s_xt, n + 1)
                    for q in range(HC):
                        last = mm(S[k][:, q * P:(q + 1) * P], w1c[:, k, q * P:(q + 1) * P], xt[:, k, :],
                                  start=True, stop=True)
                    last.then_inc(s_h, 1)
                    if c + 1 <= ROUND:
                        expert_of(m, c + 1)
                if has(0):
                    n, k = m * ROUND + c, c % 2
                    if not has(1) and has(-2):
                        pe.wait_ge(s_ys, n - 1)
                    pe.wait_ge(s_gelu, n + 1)
                    for q in range(HC):
                        last = mm((AV, SM)[k][:, 0:D], ht[:, k, q, :], w2s[:, bass.ds(e + q * D, D)],
                                  start=(q == 0), stop=(q == HC - 1))
                    last.then_inc(s_y, 1)

            expert_turns(pe, turn)

            def tokens_of(n):
                if n >= 4:
                    pe.wait_ge(s_norm, (n - 3) * FC)
                mm(SUM[n % 4][:, :], idf[:, :], xn3all[:, n * FC * D:(n + 1) * FC * D], start=True, stop=False)

            for n in range(4):
                tokens_of(n)
            for n in range(CHUNKS):
                for k in range(TOPK):
                    pe.wait_ge(s_y2[k][n % 4], 16 * (n // 4 + 1))
                    last = mm(SUM[n % 4][:, :], idf[:, :], y2[n % 4][:, k, :], start=False, stop=(k == TOPK - 1))
                last.then_inc(s_add, 1)
                if 2 <= n and n + 2 < CHUNKS:
                    tokens_of(n + 2)

        @block.scalar
        def _(act):
            act.wait_ge(s_ready, 1)
            act.activation(gexp[:, :], half[:, :], ACT.Copy)

            def move(dst, src, s, **kw):
                act.activation(dst, src, ACT.Copy).then_inc(s, 1)

            def exps(g, t, j):
                act.wait_ge(s_st, done(g, t, NJ, j))
                if not is_zero(g, t):
                    act.wait_ge(s_av, done(g, t, NJ, j) - NJ)
                n = keys(t)
                act.activation(prob[0:n, j, :], ST[j % 2][0:n, :], ACT.Exp, scale=SCALE).then_inc(s_exp, 1)

            def small(what, g, t, ended=False):
                act.wait_ge(s_sm, sm_count(g, t, what, ended))
                if what == "maxima":
                    move(nmt[:, :], SMb, s_smf)
                else:
                    move(onormt[:, :], SM[:, 0:L], s_smf)

            def sums_out(g, t):
                act.wait_ge(s_av, done(g, t, NJ, NJ - 1))
                move(ots[:, :], AV[:, :], s_ot)

            def high_part(g, k):
                act.wait_ge(s_sum, g * 2 + k + 1)
                act.activation(rhi[:, k, :], rsum[:, k, :], ACT.Copy).then_inc(s_rhi, 1)

            def work(ph, g, name):
                bank, c = ph.item(name)
                w = W[bank]
                if name in ("q", "rq", "k", "rk", "gk0", "gk1", "gk2", "gk3", "log", "pos"):
                    return
                act.wait_ge(s_w[bank], c)
                if name == "xnt":
                    move(xnt[:, :], w[:, :], s_wf[bank])
                elif name == "v":
                    move(va[:, :, :, 0:HD].rearrange("p i h c -> p (i h) c"),
                         w[:, :].rearrange("p (n c) -> p n c", c=HD), s_wf[bank])
                elif name in ("gq0", "gq1", "gq2", "gq3"):
                    move(qs[:, int(name[2]), :], w[:, :], s_wf[bank])
                elif name == "k2":
                    act.activation(k2hi[:, :], w[:, 0:CTOK], ACT.Identity, bias=bcross[:, 1:2]).then_inc(s_k2hi, 1)
                elif name == "v2":
                    act.activation(va2[0:LC, :, :, 0:HD].rearrange("p i h c -> p (i h) c"),
                                   w[0:LC, :].rearrange("p (n c) -> p n c", c=HD), ACT.Copy).then_inc(s_wf[bank], 1)
                elif name.startswith("gk2"):
                    move(k2s[:, int(name[3]), :], w[:, 0:CTOK], s_wf[bank])
                elif name.startswith("x2t"):
                    move(x2t[:, :], w[:, 0:L], s_wf[bank])
                elif name.startswith("q2"):
                    act.activation(q2hi[:, :], w[:, 0:L], ACT.Identity, bias=bcross[:, 0:1]).then_inc(s_q2hi, 1)
                elif name.startswith("gq2"):
                    move(q2s[:, int(name[3]), :, :].rearrange("p b l -> p (b l)"), w[:, :], s_wf[bank])
                elif name.startswith("x3t"):
                    i = int(name[3])
                    act.activation(pay[:, i, 1, 0:D], pay[:, i, 0, 0:D], ACT.Copy).then_inc(s_copy, 1)
                    move(xn3t[:, i * L:(i + 1) * L], w[:, 0:L], s_wf[bank])

            def step(ph, g, gp, t):
                if not is_first(ph, t):
                    sums_out(*prv(g, gp, t))
                for j in range(NJ):
                    exps(g, t, j)
                    if j == 1 and not is_first(ph, t):
                        small("normed", *prv(g, gp, t))
                    if ph.kind == "body" and (t, j) in ((3, 3), (4, 2)):
                        high_part(g + 1, t - 3)
                    if j == 3 and t == 1 and gp is not None:
                        act.wait_ge(s_gap, gp + 1)
                        act.activation(gexp[:, :], gap[:, :], ACT.Exp).then_inc(s_gexp, 1)
                    for name, kind in ph.at(t, j):
                        work(ph, group_of(kind, g, gp), name)
                if not is_last(ph, t):
                    small("maxima", *nxt(g, t))

            before = Phase("before", 0)
            for name, _ in NEXT_ITEMS:
                if name == "v":
                    act.wait_ge(s_set, SET_STEPS)
                work(before, 0, name)
                if name in ("rq", "rk"):
                    high_part(0, ("rq", "rk").index(name))
            small("maxima", 0, 0)
            act.wait_ge(s_const, 16 * len(CONSTS))
            after = all_steps(act, step)
            sums_out(NG - 1, INST - 1)
            small("normed", NG - 1, INST - 1, ended=True)
            for name, _ in TAIL_ITEMS:
                work(after, NG - 1, name)
            act.wait_ge(s_gap, NG)
            act.activation(gexp[:, :], gap[:, :], ACT.Exp).then_inc(s_gexp, 1)
            act.activation(onormt[:, 0:GS], half[:, :], ACT.Gelu)
            act.wait_ge(s_tab, 1)

            def turn(m, c, has):
                if has(1):
                    n, k = m * ROUND + c + 1, (c + 1) % 2
                    b = act.value_load(tab[0:1, 2, bass.ds(n, 1)], min_val=0, max_val=(E - 1) * HC)
                    act.wait_ge(s_h, n + 1)
                    if has(-1):
                        act.wait_ge(s_y, n - 1)
                    for q in range(HC):
                        last = act.activation(ht[:, k, q, :], S[k][:, q * P:(q + 1) * P], ACT.Gelu,
                                              bias=b1s[:, bass.ds(b + q, 1)])
                    last.then_inc(s_gelu, 1)

            expert_turns(act, turn)

            for i in range(SEQS):
                if i % FC == 0:
                    act.wait_ge(s_rsfm, i // FC + 1)
                r = SUM[(i // FC) % 4][:, (i % FC) * D:(i % FC + 1) * D]
                act.activation(xn3all[:, i * D:(i + 1) * D], r, ACT.Identity,
                               bias=rsf[:, 1, i:i + 1], scale=rsf[:, 0, i:i + 1]).then_inc(s_norm, 1)

        @block.vector
        def _(dve):
            V = nc.vector
            dve.wait_ge(s_ready, 1)

            def bias_rows():
                dve.wait_ge(s_const, 16 * len(CONSTS))
                V.tensor_scalar(bvb[:, 0, :], idf[:, :], 0.0, bself[:, 4:5], ALU.mult, ALU.add).then_inc(s_bvb, 1)
                V.tensor_scalar(bvb[:, 1, :], idf[:, :], 0.0, bcross[:, 2:3], ALU.mult, ALU.add).then_inc(s_bvb, 1)
                dve.wait_ge(s_cbp, 2)
                V.tensor_tensor(cself[:, :], S[0][:, 0:D], bprow[:, :], ALU.add).then_inc(s_cb, 1)
                V.tensor_tensor(ccross[:, :], S[1][:, 0:D], borow[:, :], ALU.add).then_inc(s_cb, 1)

            def statistics(g):
                wait_alone(dve, s_x, g * 16 + 16)
                for i in range(GS):
                    V.bn_stats(st1[:, i, :], xin[:, i, :]).then_inc(s_raw1, 1)
                wait_alone(dve, s_raw1, g * GS + GS)
                for i in range(GS):
                    V.bn_aggr(mv1[:, i, :], st1[:, i, :]).then_inc(s_st1, 1)

            def normed_group(g):
                wait_alone(dve, s_nrm1, g * 2 + 2)
                for i in range(GS):
                    V.tensor_scalar(xn1[:, i, :], xin[:, i, :], mv1[:, i, 0:1], rs1[:, i:i + 1],
                                    ALU.subtract, ALU.mult).then_inc(s_xn1, 1)

            def maxima(g, t, j):
                n = keys(t)
                dve.wait_ge(s_S, done(g, t, NJ, j))
                V.tensor_reduce(nm[:, j, :], S[j % 2][:, 0:NB * n].rearrange("p (b k) -> p b k", b=NB),
                                AX.X, ALU.max, negate=True).then_inc(s_max, 1)

            def maxima_parts(g, t, last=None):
                dve.wait_ge(s_max, done(g, t, NJ, NJ - 1))
                if last:
                    dve.wait_ge(s_sm, sm_count(*last, "maxima"))
                V.tensor_copy(nmp[:, :, 0:NB], nm[:, :, :]).then_inc(s_neg, 1)
                dve.wait_ge(s_neg, done(g, t))
                V.tensor_tensor(nmp[:, :, NB:2 * NB], nm[:, :, :], nmp[:, :, 0:NB], ALU.subtract).then_inc(s_nmp, 1)

            def norm_rows(g, t, ended=False):
                dve.wait_ge(s_sm, sm_count(g, t, "sums", ended))
                o = SM[:, :].rearrange("p (h c) -> p h c", c=VW)
                V.reciprocal(rden[:, :], o[:, :, HD:HD + 1].rearrange("p h c -> p (h c)")).then_inc(s_rden, 1)
                dve.wait_ge(s_rden, done(g, t))
                V.tensor_tensor(onorm[:, :, :], o[:, :, 0:HD],
                                rden[:, :].unsqueeze(2).to_broadcast([P, H, HD]), ALU.mult).then_inc(s_smf, 1)

            def residual(g, t, ended=False):
                dve.wait_ge(s_sm, sm_count(g, t, "projected", ended))
                i = t % GS
                if t < GS:
                    dve.wait_ge(s_xfree, g + 1)
                    row, more = x1[:, i, :], xc[:, i, :]
                else:
                    if t == GS:
                        dve.wait_ge(s_keep, g * 32 + 16)
                    dve.wait_ge(s_x1c, g * GS + i + 1)
                    row, more = x2g[:, i, :], x1c[:, i, :]
                V.tensor_tensor(row, SM[:, 0:D], more, ALU.add).then_inc(s_smf, 1)

            def residual_statistics(g, t, ended=False):
                i = t % GS
                row = x1[:, i, :] if t < GS else x2g[:, i, :]
                wait_alone(dve, s_smf, sm_count(g, t, "projected", ended))
                V.bn_stats(st2[:, :], row).then_inc(s_raw2, 1)
                if not is_zero(g, t):
                    wait_alone(dve, s_xn2, done(g, t) - 1)
                wait_alone(dve, s_raw2, done(g, t))
                V.bn_aggr(mv2[:, :], st2[:, :]).then_inc(s_x1, 1)

            def work(ph, g, name):
                bank, c = ph.item(name)
                w = W[bank]
                w3 = w[:, :].rearrange("p (i l) -> p i l", i=GS)
                if name in ("q", "rq", "k", "rk"):
                    n = ("q", "rq", "k", "rk").index(name)
                    table, to = (sinb, rb) if n % 2 else (cosb, ra)
                    dve.wait_ge(s_w[bank], c)
                    V.scalar_tensor_tensor(
                        to[:, n // 2, :].rearrange("p (i l) -> p i l", i=GS), w3, bself[:, n:n + 1],
                        table[:, :].unsqueeze(1).to_broadcast([P, GS, L]), ALU.add, ALU.mult).then_inc(s_wf[bank], 1)
                    if n % 2:
                        for half_item in (("q", "rq"), ("k", "rk"))[n // 2]:
                            fb, fc = ph.item(half_item)
                            dve.wait_ge(s_wf[fb], fc)
                        V.tensor_tensor(rsum[:, n // 2, :], ra[:, n // 2, :], rb[:, n // 2, :], ALU.add).then_inc(s_sum, 1)
                elif name in ("gk0", "gk1", "gk2", "gk3"):
                    dve.wait_ge(s_w[bank], c)
                    V.tensor_copy(ks[:, int(name[2]), :], w[:, :]).then_inc(s_wf[bank], 1)
                elif name == "k2":
                    dve.wait_ge(s_k2hi, g + 1)
                    V.scalar_tensor_tensor(k2lo[:, :], w[:, 0:CTOK], bcross[:, 1:2], k2hi[:, :],
                                           ALU.add, ALU.subtract).then_inc(s_wf[bank], 1)
                elif name in ("q20", "q21", "q22", "q23"):
                    dve.wait_ge(s_q2hi, g * GS + int(name[2]) + 1)
                    V.scalar_tensor_tensor(q2lo[:, :], w[:, 0:L], bcross[:, 0:1], q2hi[:, :],
                                           ALU.add, ALU.subtract).then_inc(s_wf[bank], 1)
                elif name == "log":
                    choose(g, w, bank, c)
                elif name == "pos":
                    place(g, w, bank, c)

            CHOOSE = 2 * GS + 2

            def routed_step(g, n, ins, alone=False, wait=True):
                ins.then_inc(s_route, 1)
                if wait and alone:
                    wait_alone(dve, s_route, g * CHOOSE + n)
                elif wait:
                    dve.wait_ge(s_route, g * CHOOSE + n)

            def choose(g, w, bank, c):
                dve.wait_ge(s_w[bank], c)
                V.tensor_tensor(lg[:, :, :], w[:, 0:GS * E].rearrange("p (i e) -> p i e", e=E),
                                bgrow[:, :].unsqueeze(1).to_broadcast([P, GS, E]), ALU.add).then_inc(s_wf[bank], 1)
                wait_alone(dve, s_wf[bank], c)
                for i in range(GS):
                    routed_step(g, i + 1, V.max(top[:, i, :], lg[:, i, :]), alone=True, wait=(i == GS - 1))
                for i in range(GS):
                    routed_step(g, GS + i + 1, V.max_index(topi[:, i, :], top[:, i, :], lg[:, i, :]), wait=False)

            def mark(g):
                n = 2 * GS
                dve.wait_ge(s_route, g * CHOOSE + n)
                routed_step(g, n + 1, V.tensor_copy(topf[:, :, :], topi[:, :, 0:TOPK]))
                routed_step(g, n + 2, V.tensor_tensor(
                    hot[:, :, :, :], iota8.unsqueeze(1).unsqueeze(1).to_broadcast([P, GS, TOPK, E]),
                    topf[:, :, :].unsqueeze(3).to_broadcast([P, GS, TOPK, E]), ALU.is_equal))
                V.tensor_tensor(hotb[:, :, :], hot[:, :, 0, :], hot[:, :, 1, :], ALU.add).then_inc(s_hot, 1)
                V.tensor_tensor(gap[:, :], top[:, :, 1], top[:, :, 0], ALU.subtract).then_inc(s_gap, 1)

            def place(g, w, bank, c):
                dve.wait_ge(s_w[bank], c)
                V.tensor_tensor(slot[:, :, :], w[:, 0:GS * E].rearrange("p (i e) -> p i e", e=E),
                                ebaser.unsqueeze(1).to_broadcast([P, GS, E]), ALU.add).then_inc(s_wf[bank], 1)
                V.tensor_copy(pay[:, :, :, D + 1].bitcast(I32), rowid[:, bass.ds(g * GS, GS), :]).then_inc(s_rowid, 1)

            def place_last():
                n = 0

                def did(ins):
                    nonlocal n
                    n += 1
                    ins.then_inc(s_last, 1)
                    dve.wait_ge(s_last, n)

                bank, c = after.item("pos")
                dve.wait_ge(s_wf[bank], c)
                did(V.tensor_tensor(picked[:, :, :, :], hot[:, :, :, :],
                                    slot[:, :, :].unsqueeze(2).to_broadcast([P, GS, TOPK, E]), ALU.mult))
                did(V.tensor_reduce(destf[:, :, :], picked[:, :, :, :], AX.X, ALU.add))
                V.tensor_copy(dest[:, :, :], destf[:, :, :])
                dve.wait_ge(s_gexp, NG)
                did(V.tensor_scalar(gden[:, :], gexp[:, :], 1.0, None, ALU.add))
                did(V.reciprocal(pay[:, :, 0, D], gden[:, :]))
                V.tensor_tensor(pay[:, :, 1, D], gexp[:, :], pay[:, :, 0, D], ALU.mult).then_inc(s_pay, 1)

            EARLY = (0,)

            def step(ph, g, gp, t):
                for j in range(NJ):
                    if not is_last(ph, t):
                        maxima(*nxt(g, t), j)
                    if not is_first(ph, t) and j == 2:
                        residual(*prv(g, gp, t))
                        if t in EARLY:
                            residual_statistics(*prv(g, gp, t))
                    if t == 1 and j == 3 and gp is not None:
                        mark(gp)
                    if t == 2 and j == 1 and ph.kind == "body":
                        statistics(g + 1)
                    if not is_first(ph, t) and j == 0:
                        norm_rows(*prv(g, gp, t))
                    if j == NJ - 1 and not is_last(ph, t):
                        maxima_parts(*nxt(g, t), last=(g, t))
                    if j == 3 and not is_first(ph, t) and t not in EARLY:
                        residual_statistics(*prv(g, gp, t))
                    if t == 2 and j == 3 and ph.kind == "body":
                        normed_group(g + 1)
                    for name, kind in ph.at(t, j):
                        work(ph, group_of(kind, g, gp), name)

            before = Phase("before", 0)
            statistics(0)
            normed_group(0)
            dve.wait_ge(s_first, 16 * len(FIRST))
            for name, _ in NEXT_ITEMS:
                work(before, 0, name)
                if name == "rk":
                    bias_rows()
            dve.wait_ge(s_set, SET_STEPS)
            for j in range(NJ):
                maxima(0, 0, j)
            maxima_parts(0, 0)
            after = all_steps(dve, step)
            norm_rows(NG - 1, INST - 1, ended=True)
            residual(NG - 1, INST - 1, ended=True)
            residual_statistics(NG - 1, INST - 1, ended=True)
            for name, _ in TAIL_ITEMS:
                if name == "pos":
                    mark(NG - 1)
                work(after, NG - 1, name)
            place_last()

            nt = 0

            def did(ins):
                nonlocal nt
                ins.then_inc(s_tabs, 1)
                nt += 1
                dve.wait_ge(s_tabs, nt)

            dve.wait_ge(s_cnt, 1)
            did(V.tensor_copy(counts[:, :], S[0][0:1, 0:E]))
            V.tensor_copy(countsi[:, :], counts[:, :]).then_inc(s_cnti, 1)
            did(V.memset(ones8[:, :], 1.0))
            did(V.tensor_tensor(over[:, :, :], counts[:, :].unsqueeze(2).to_broadcast([1, E, SEQS]),
                                edges[:, 0:SEQS].unsqueeze(1).to_broadcast([1, E, SEQS]), ALU.is_gt))
            did(V.tensor_reduce(tiles[:, 0, :], over[:, :, :], AX.X, ALU.add))
            did(V.tensor_tensor_scan(tiles[:, 1, :], ones8[:, :], tiles[:, 0, :], 0.0, ALU.mult, ALU.add))
            did(V.tensor_scalar(tiles[:, 2, :], tiles[:, 0, :], -float(P), float(REGION), ALU.mult, ALU.add))
            number = edges[:, SEQS:SEQS + NT]
            did(V.tensor_tensor(isof[:, 0, :, :], number.unsqueeze(2).to_broadcast([1, NT, E]),
                                tiles[:, 1, :].unsqueeze(1).to_broadcast([1, NT, E]), ALU.is_ge))
            did(V.tensor_tensor(isof[:, 1, :, :], isof[:, 0, :, :],
                                tiles[:, 2, :].unsqueeze(1).to_broadcast([1, NT, E]), ALU.mult))
            did(V.tensor_reduce(tabf[:, 2, :], isof[:, 0, :, :], AX.X, ALU.add))
            did(V.tensor_reduce(tabf[:, 1, :], isof[:, 1, :, :], AX.X, ALU.add))
            did(V.tensor_scalar(tabf[:, 3, :], tabf[:, 2, :], float(E - 1), None, ALU.is_le))
            did(V.tensor_scalar(tabf[:, 0, :], number, float(P), -float(SPARE), ALU.mult, ALU.add))
            did(V.tensor_tensor(tabf[:, 0, :], tabf[:, 0, :], tabf[:, 1, :], ALU.add))
            did(V.tensor_tensor(tabf[:, 0, :], tabf[:, 0, :], tabf[:, 3, :], ALU.mult))
            did(V.tensor_scalar(tabf[:, 2, :], tabf[:, 2, :], float(E - 1), None, ALU.min))
            did(V.tensor_scalar(tabf[:, 1, :], tabf[:, 0, :], float(SPARE), None, ALU.add))
            did(V.tensor_scalar(tabf[:, 0, :], tabf[:, 2, :], float(HID), None, ALU.mult))
            did(V.tensor_scalar(tabf[:, 3, :], tabf[:, 2, :], float(D), None, ALU.mult))
            did(V.tensor_scalar(tabf[:, 2, :], tabf[:, 2, :], float(HC), None, ALU.mult))
            V.tensor_copy(tab[:, :, :], tabf[:, :, :]).then_inc(s_tab, 1)
            dve.wait_ge(s_tab, 1)

            experts = {}

            def expert_of(m, c):
                if c not in experts:
                    experts[c] = dve.value_load(tab[0:1, 3, bass.ds(m * ROUND + c, 1)], min_val=0, max_val=(E - 1) * D)
                return experts[c]

            def turn(m, c, has):
                if c == 1:
                    experts.clear()
                if has(2):
                    n, k = m * ROUND + c + 2, (c + 2) % 2
                    e = expert_of(m, c + 2)
                    if has(0) and not has(-1):
                        dve.wait_ge(s_h, n - 1)
                    V.tensor_copy(w1c[:, k, :], w1s[:, bass.ds(e * (HID // D), HID)])
                    dve.wait_ge(s_xp, n + 1)
                    V.tensor_copy(xt[:, k, :], W[k][:, 0:P]).then_inc(s_xt, 1)
                    if has(3) and c + 1 <= ROUND:
                        expert_of(m, c + 3)
                if has(0):
                    n, k, r = m * ROUND + c, c % 2, c % ROUND
                    e = expert_of(m, c)
                    dve.wait_ge(s_y, n + 1)
                    V.tensor_tensor(ys[:, k, :], (AV, SM)[k][:, 0:D], b2row[:, bass.ds(e, D)], ALU.add).then_inc(s_ys, 1)
                    dve.wait_ge(s_ys, n + 1)
                    if has(-4):
                        dve.wait_ge(s_sc[c % 4], (m * 2 + c // 4) * 16)
                    V.tensor_scalar(yw[:, c % 4, :], ys[:, k, :], xr[:, r, D:D + 1], None, ALU.mult).then_inc(s_yw, 1)

            expert_turns(dve, turn)

            def chunk_statistics(n):
                dve.wait_ge(s_add, n + 1)
                for i in range(FC):
                    V.bn_stats(stf[:, n * FC + i, :], SUM[n % 4][:, i * D:(i + 1) * D]).then_inc(s_rawf, 1)
                dve.wait_ge(s_rawf, (n + 1) * FC)
                for i in range(n * FC, (n + 1) * FC):
                    V.bn_aggr(mvf[:, i, :], stf[:, i, :]).then_inc(s_stf, 1)
                dve.wait_ge(s_stf, (n + 1) * FC)
                V.tensor_scalar(nmf[:, n * FC:(n + 1) * FC], mvf[:, n * FC:(n + 1) * FC, 0], -1.0, None, ALU.mult).then_inc(s_nmean, 1)

            def chunk_out(n):
                at = slice(n * FC * D, (n + 1) * FC * D)
                if n % 2:
                    dve.wait_ge(s_gam[1], n // 2 + 1)
                else:
                    dve.wait_ge(s_norm, (n + 1) * FC)
                    times_gamma(V, n)
                    dve.wait_ge(s_gam[0], n // 2 + 1)
                dve.wait_ge(s_xb, n + 1)
                V.tensor_tensor(x2all[:, at], xn3all[:, at], x2all[:, at], ALU.add).then_inc(s_fin, 1)

            for n in range(CHUNKS + 2):
                if n < CHUNKS:
                    chunk_statistics(n)
                if n >= 2:
                    chunk_out(n - 2)

        @block.gpsimd
        def _(pool):
            G = nc.gpsimd
            G.memset(half[:, :], -0.5).then_inc(s_ready, 1)
            pool.wait_ge(s_ready, 1)
            G.memset(va[:, :, :, :], 0.0).then_inc(s_set, 1)
            G.memset(minus1[:, :], -1.0).then_inc(s_set, 1)
            G.memset(halff[:, :], -0.5).then_inc(s_set, 1)

            def set_up():
                pool.dma_start(filler[:, :], fill).then_inc(s_scat, 16)
                G.memset(va2[:, :, :, :], 0.0).then_inc(s_set, 1)
                G.memset(nmp[:, :, :], 0.0).then_inc(s_set, 1)
                G.memset(onesb[:, :], 1.0).then_inc(s_set, 1)
                G.memset(seenb[:, :], 0.0).then_inc(s_set, 1)
                G.memset(seen[:, :], 0.0).then_inc(s_seen, 1)
                pool.wait_ge(s_set, SET_STEPS - 2)
                G.memset(va[:, :, :, HD], 1.0).then_inc(s_set, 1)
                G.memset(va2[:, :, :, HD], 1.0).then_inc(s_set, 1)
                G.memset(pay[:, :, :, :], 0.0).then_inc(s_none, 1)
                G.memset(destf[:, :, :], float(SPARE)).then_inc(s_none, 1)
                pool.wait_ge(s_none, 2)
                G.tensor_copy(dest[:, :, :], destf[:, :, :]).then_inc(s_pay, 1)

            def norm_group(g):
                wait_alone(pool, s_st1, g * GS + GS)
                G.tensor_scalar(ve1[:, :], mv1[:, :, 1], EPS, None, ALU.add).then_inc(s_nrm1, 1)
                wait_alone(pool, s_nrm1, g * 2 + 1)
                G.tensor_tensor(rs1[:, :], ve1[:, :], half[:, :], ALU.pow).then_inc(s_nrm1, 1)

            def add_bias(g):
                wait_alone(pool, s_xn1, g * GS + GS)
                G.tensor_tensor(xc[:, :, :], xin[:, :, :], cself[:, :].unsqueeze(1).to_broadcast([P, GS, D]),
                                ALU.add).then_inc(s_xfree, 1)

            def parts(g, k):
                wait_alone(pool, s_rhi, g * 2 + k + 1)
                G.tensor_tensor(rlo[:, k, :], rsum[:, k, :], rhi[:, k, :], ALU.subtract).then_inc(s_parts, 1)

            def norm_instance(g, t):
                i = t % GS
                wait_alone(pool, s_x1, done(g, t))
                G.tensor_scalar(ve2[:, :], mv2[:, 1:2], EPS, None, ALU.add).then_inc(s_nrm2, 1)
                wait_alone(pool, s_nrm2, g * (2 * INST) + 2 * t + 1)
                G.tensor_tensor(rs2[:, :], ve2[:, :], half[:, 0:1], ALU.pow).then_inc(s_nrm2, 1)
                wait_alone(pool, s_nrm2, g * (2 * INST) + 2 * t + 2)
                if t < GS:
                    G.tensor_scalar(xn2[:, i, :], x1[:, i, :], mv2[:, 0:1], rs2[:, :],
                                    ALU.subtract, ALU.mult).then_inc(s_xn2, 1)
                    G.tensor_tensor(x1c[:, i, :], x1[:, i, :], ccross[:, :], ALU.add).then_inc(s_x1c, 1)
                else:
                    if i == 0:
                        wait_alone(pool, s_scat, (g + 1) * (16 * GS * TOPK) + 16)
                        wait_alone(pool, s_keep, g * 32 + 16)
                    G.tensor_scalar(pay[:, i, 0, 0:D], x2g[:, i, :], mv2[:, 0:1], rs2[:, :],
                                    ALU.subtract, ALU.mult).then_inc(s_xn2, 1)

            PLACE = 10

            def place_tokens(ph, g):
                n = 0

                def did(ins):
                    nonlocal n
                    n += 1
                    ins.then_inc(s_place, 1)
                    wait_alone(pool, s_place, g * PLACE + n)

                wait_alone(pool, s_gexp, g + 1)
                did(G.tensor_scalar(gden[:, :], gexp[:, :], 1.0, None, ALU.add))
                did(G.tensor_tensor(pay[:, :, 0, D], gden[:, :], minus1[:, :], ALU.pow))
                did(G.tensor_tensor(pay[:, :, 1, D], gexp[:, :], pay[:, :, 0, D], ALU.mult))
                bank, c = ph.item("pos")
                wait_alone(pool, s_wf[bank], c)
                wait_alone(pool, s_rowid, g + 1)
                wait_alone(pool, s_copy, g * GS + GS)
                did(G.tensor_tensor(gsum[:, :, :], hotb[:, 0:2, :], hotb[:, 2:4, :], ALU.add))
                did(G.tensor_tensor(seen[:, :], seen[:, :], gsum[:, 0, :], ALU.add))
                did(G.tensor_tensor(seen[:, :], seen[:, :], gsum[:, 1, :], ALU.add))
                G.tensor_copy(seenb[:, :], seen[:, :]).then_inc(s_seen, 1)
                did(G.tensor_tensor(picked[:, :, :, :], hot[:, :, :, :],
                                    slot[:, :, :].unsqueeze(2).to_broadcast([P, GS, TOPK, E]), ALU.mult))
                did(G.tensor_tensor(picked[:, :, :, 0:4], picked[:, :, :, 0:4], picked[:, :, :, 4:8], ALU.add))
                did(G.tensor_tensor(picked[:, :, :, 0:2], picked[:, :, :, 0:2], picked[:, :, :, 2:4], ALU.add))
                did(G.tensor_tensor(destf[:, :, :], picked[:, :, :, 0], picked[:, :, :, 1], ALU.add))
                G.tensor_copy(dest[:, :, :], destf[:, :, :]).then_inc(s_pay, 1)
                assert n == PLACE

            def scatter(g, some):
                wait_alone(pool, s_pay, g + 1)
                for i in some:
                    for k in range(TOPK):
                        pool.indirect_dma_start(
                            out=routed, out_offset=bass.IndirectOffsetOnAxis(ap=dest[:, i, k:k + 1].bitcast(U32), axis=0),
                            in_=pay[:, i, k, :], in_offset=None, bounds_check=SPARE - 1, oob_is_err=False).then_inc(s_scat, 16)

            def step(ph, g, gp, t):
                if ph.kind == "body":
                    if t == 2:
                        norm_group(g + 1)
                    if t in (4, 5):
                        parts(g + 1, t - 4)
                if not is_first(ph, t):
                    norm_instance(*prv(g, gp, t))
                if t == 1 and gp is not None:
                    place_tokens(ph, gp)
                if ph.kind == "body" and t == 5:
                    add_bias(g + 1)
                if t in (3, 4):
                    scatter(g, range(2 * (t - 3), 2 * (t - 2)))

            norm_group(0)
            set_up()
            for k in range(2):
                parts(0, k)
            pool.wait_ge(s_cb, 2)
            add_bias(0)
            all_steps(pool, step)
            norm_instance(NG - 1, INST - 1)
            wait_alone(pool, s_copy, NG * GS)
            scatter(NG, range(GS))

            pool.wait_ge(s_keep, 32 * NG + 16)
            wait_alone(pool, s_fill, 16 * (E + 1))
            for n in range(CHUNKS):
                r = x2all[:, n * FC * D:(n + 1) * FC * D].rearrange("p (s d) -> p s d", d=D)
                G.tensor_tensor(r, r, betar[:, :].unsqueeze(1).to_broadcast([P, FC, D]), ALU.add).then_inc(s_xb, 1)

            def turn(m, c, has):
                if has(0):
                    wait_alone(pool, s_yw, m * ROUND + c + 1)
                    pool.indirect_dma_start(
                        out=expert_out,
                        out_offset=bass.IndirectOffsetOnAxis(ap=xr[:, c % ROUND, D + 1:D + 2].bitcast(U32), axis=0),
                        in_=yw[:, c % 4, :], in_offset=None, bounds_check=YROWS - 1, oob_is_err=False).then_inc(s_sc[c % 4], 16)

            expert_turns(pool, turn)

            def inverse_deviations(n):
                at = slice(n * FC, (n + 1) * FC)
                pool.wait_ge(s_nmean, n + 1)
                G.tensor_scalar(rsf[:, 1, at], mvf[:, at, 1], EPS, None, ALU.add).then_inc(s_rsf, 1)
                pool.wait_ge(s_rsf, 2 * n + 1)
                G.tensor_tensor(rsf[:, 0, at], rsf[:, 1, at], halff[:, at], ALU.pow).then_inc(s_rsf, 1)
                pool.wait_ge(s_rsf, 2 * n + 2)
                G.tensor_tensor(rsf[:, 1, at], nmf[:, at], rsf[:, 0, at], ALU.mult).then_inc(s_rsfm, 1)

            for n in range(CHUNKS + 1):
                if n < CHUNKS:
                    inverse_deviations(n)
                if n and (n - 1) % 2:
                    pool.wait_ge(s_norm, n * FC)
                    times_gamma(G, n - 1)

ARRAYS = ("x", "ctx_t", "w_self", "b_self", "bp", "w_cross", "b_cross", "bo", "wg", "bg", "w1", "b1", "w2", "b2",
          "gamma", "beta", "cos_t", "sin_t", "sel_q", "sel_k", "ones_rows", "ident", "ident_bf", "upper", "ebase",
          "row_id", "tile_edge", "fill")


def layout(inputs):
    import numpy as np
    g = {k: np.asarray(v) for k, v in inputs.items()}
    bf16 = mybir.dt.np(BF16)
    swap = np.arange(D) ^ 1
    a = {"x": g["x"], "ctx_t": np.ascontiguousarray(g["ctx_1024"].transpose(2, 0, 1).reshape(D, SEQS * LC))}
    n = "L0_attn_"
    wq, wk = g[n + "Wq"], g[n + "Wk"]
    a["w_self"] = np.stack([wq, wq[:, swap], wk, wk[:, swap], g[n + "Wv"], g[n + "Wp"]], 1)
    a["b_self"] = np.stack([g[n + "bq"], g[n + "bq"][swap], g[n + "bk"], g[n + "bk"][swap], g[n + "bv"]], 1)
    a["bp"] = g[n + "bp"]
    n = "L0_xattn_"
    a["w_cross"] = np.stack([g[n + w].T for w in ("Wq", "Wk", "Wv", "Wo")], 1)
    a["b_cross"] = np.stack([g[n + b] for b in ("bq", "bk", "bv")], 1)
    a["bo"] = g[n + "bo"]
    n = "L0_ffn_"
    a["wg"], a["bg"] = g[n + "Wg"], g[n + "bg"]
    a["w1"], a["w2"], a["b2"] = g[n + "W1"], g[n + "W2"], g[n + "b2"]
    a["b1"] = g[n + "b1"].reshape(E, HC, P).transpose(2, 0, 1).reshape(P, E * HC)
    a["gamma"], a["beta"] = g[n + "gamma"], g[n + "beta"]
    inv = (np.float32(1.0) / np.float32(10000.0) ** (np.arange(0, HD, 2, dtype=np.float32) / np.float32(HD))).astype(np.float32)
    freq = np.arange(L, dtype=np.float32)[:, None] * inv
    pairs = (np.arange(D) % HD) // 2
    sign = np.where(np.arange(D) % 2, 1.0, -1.0).astype(np.float32)
    a["cos_t"] = np.cos(freq)[:, pairs].T.astype(np.float32)
    a["sin_t"] = (np.sin(freq)[:, pairs].T * sign[:, None]).astype(np.float32)
    sel = np.zeros((2, P, 2, NB, P), np.float16)
    for j in range(NJ):
        for b in range(NB):
            for c in range(4):
                for d in range(HD):
                    r, at = 32 * j + HD * c + d, (NB * j + b) * HD + d
                    sel[0, at, c // 2, b, r] = 1
                    sel[1, at, c % 2, b, r] = 1
    a["sel_q"], a["sel_k"] = sel[0], sel[1]
    rows = np.zeros((P, NJ, NB, P), bf16)
    for j in range(NJ):
        for b in range(NB):
            rows[32 * j + b, j, b, :] = rows[32 * j + NB + b, j, b, :] = 1
    a["ones_rows"] = rows
    a["ident"] = np.eye(P, dtype=np.float32)
    a["ident_bf"] = np.eye(P).astype(bf16)
    a["upper"] = np.triu(np.ones((P, P)), 1).astype(bf16)
    a["ebase"] = np.broadcast_to(np.stack([np.arange(E) * REGION, np.arange(E)]).astype(np.float32), (P, 2, E))
    token = np.arange(SEQS)[None, :, None] * L + np.arange(P)[:, None, None]
    a["row_id"] = (token + np.arange(TOPK)[None, None, :] * NTOK).astype(np.int32)
    a["tile_edge"] = np.concatenate([np.arange(SEQS) * P, np.arange(NT)]).astype(np.float32)[None]
    fill = np.zeros((P, PAYW), np.float32)
    fill[:, D + 1] = np.full(P, YROWS, np.int32).view(np.float32)
    a["fill"] = fill
    return {k: np.ascontiguousarray(a[k]) for k in ARRAYS}


def kernel(**inputs):
    import concourse.bacc as _bacc
    from concourse import mybir as _mybir
    from concourse.bass_utils import run_bass_kernel_spmd as _run

    arrays = layout(inputs)
    nc = _bacc.Bacc("TRN2", target_bir_lowering=False, num_devices=1)
    args = [nc.dram_tensor(n, a.shape, _mybir.dt.from_np(a.dtype), kind="ExternalInput").ap() for n, a in arrays.items()]
    args.append(nc.dram_tensor("out", (SEQS, L, D), F32, kind="ExternalOutput").ap())
    decoder_layer(nc, *args)
    return _run(nc, [arrays], core_ids=[0]).results[0]["out"]
```
